# Optimizing a Trainium2 kernel written in Bass

```python
import numpy as np
import jax
import jax.numpy as jnp

def _softmax(x, axis=-1):
    return jax.nn.softmax(x, axis=axis)

def _gelu(x):
    return jax.nn.gelu(x, approximate=True)

def _silu(x):
    return jax.nn.silu(x)

def _sigmoid(x):
    return jax.nn.sigmoid(x)

def _layernorm(x, axis=-1, eps=1e-05):
    m = jnp.mean(x, axis=axis, keepdims=True)
    v = jnp.var(x, axis=axis, keepdims=True)
    return (x - m) / jnp.sqrt(v + eps)

def _scatter_add(tgt, idx, src, axis=0):
    return tgt.at[idx].add(src)

def _segment_sum(src, seg, n):
    return jax.ops.segment_sum(src, seg, n)
kernel_name = 'mk_gnn_preln_d4_gnn_r8_410365'

def setup_inputs(seed: int=0):
    np.random.seed(seed)
    _w = jnp.asarray

    def _rec_inputs():
        import jax
        import jax.numpy as jnp
        _gk = jax.random.key(seed)
        x = -0.0005121 + 1.001 * jax.random.normal(jax.random.fold_in(_gk, 1), (6250, 64), jnp.float32)
        src = jax.random.randint(jax.random.fold_in(_gk, 2), (200000,), 0, 6250, jnp.int32)
        dst = jnp.minimum((6250 * jax.random.uniform(jax.random.fold_in(_gk, 3), (200000,)) ** 2.0).astype(jnp.int32), 49999)
        _o = jnp.argsort(dst, stable=True)
        src = src[_o]
        dst = dst[_o]
        edge_attr_16 = -0.00010739 + 0.99994 * jax.random.normal(jax.random.fold_in(_gk, 12), (200000, 16), jnp.float32)
        edge_attr_32 = 0.000189758 + 1.00013 * jax.random.normal(jax.random.fold_in(_gk, 13), (200000, 32), jnp.float32)
        return (x, src, dst, edge_attr_16, edge_attr_32)
    x, src, dst, edge_attr_16, edge_attr_32 = _rec_inputs()

    def _L0_gnn_setup():
        import jax, jax.numpy as jnp
        import numpy as np
        N_NODES = 6250
        N_EDGES = 100000
        D_NODE = 64
        D_EDGE = 16
        D_HID = 64
        N_LAYERS = 3
        EPS = 1e-05

        def _ln(x):
            m = jnp.mean(x, axis=-1, keepdims=True)
            v = jnp.mean(jnp.square(x - m), axis=-1, keepdims=True)
            return (x - m) * jax.lax.rsqrt(v + EPS)

        def _ffn(x, w, b):
            return jax.nn.relu(_ln(x @ w + b))
        key = jax.random.key(seed)
        ks = jax.random.split(key, 10)
        d_msg_in = 2 * D_NODE + D_EDGE
        d_upd_in = D_NODE + D_HID
        s = 0.05
        return {'node_features': jax.random.normal(ks[0], (N_NODES, D_NODE), jnp.float32), 'edge_features': jax.random.normal(ks[1], (N_EDGES, D_EDGE), jnp.float32), 'edge_index': jax.random.randint(ks[2], (2, N_EDGES), 0, N_NODES), 'msg_w1': jax.random.normal(ks[3], (N_LAYERS, d_msg_in, D_HID), jnp.float32) * s, 'msg_b1': jnp.zeros((N_LAYERS, D_HID), jnp.float32), 'msg_w2': jax.random.normal(ks[4], (N_LAYERS, D_HID, D_HID), jnp.float32) * s, 'msg_b2': jnp.zeros((N_LAYERS, D_HID), jnp.float32), 'upd_w': jax.random.normal(ks[5], (N_LAYERS, d_upd_in, D_HID), jnp.float32) * s, 'upd_b': jnp.zeros((N_LAYERS, D_HID), jnp.float32)}
    _L0_gnn_all = _L0_gnn_setup()
    _L0_gnn_in = {k: v for k, v in _L0_gnn_all.items() if k in ('msg_w1', 'msg_b1', 'msg_w2', 'msg_b2', 'upd_w', 'upd_b')}
    del _L0_gnn_all

    def _L1_gnn_setup():
        import jax, jax.numpy as jnp
        import numpy as np
        N_NODES = 12500
        N_EDGES = 200000
        NODE_F = 64
        EDGE_F = 32
        BN_EPS = 1e-05
        key = jax.random.key(seed)
        ks = jax.random.split(key, 8)
        in_dim = 2 * NODE_F + EDGE_F
        scale = 1.0 / np.sqrt(in_dim)
        return {'node_attrs': jax.random.normal(ks[0], (N_NODES, NODE_F), jnp.float32), 'edge_index': jax.random.randint(ks[1], (2, N_EDGES), 0, N_NODES, jnp.int64), 'edge_attrs': jax.random.normal(ks[2], (N_EDGES, EDGE_F), jnp.float32), 'W_f': jax.random.normal(ks[3], (in_dim, NODE_F), jnp.float32) * scale, 'b_f': jnp.zeros((NODE_F,), jnp.float32), 'W_s': jax.random.normal(ks[4], (in_dim, NODE_F), jnp.float32) * scale, 'b_s': jnp.zeros((NODE_F,), jnp.float32), 'gamma': jnp.ones((NODE_F,), jnp.float32), 'beta': jnp.zeros((NODE_F,), jnp.float32)}
    _L1_gnn_all = _L1_gnn_setup()
    _L1_gnn_in = {k: v for k, v in _L1_gnn_all.items() if k in ('W_f', 'b_f', 'W_s', 'b_s', 'gamma', 'beta')}
    del _L1_gnn_all

    def _L2_gnn_setup():
        import jax, jax.numpy as jnp
        import numpy as np
        N_NODES = 12500
        N_EDGES = 156250
        D_FEAT = 64
        key = jax.random.key(seed)
        kx, ke = jax.random.split(key)
        x = jax.random.normal(kx, (N_NODES, D_FEAT), dtype=jnp.float32)
        edge_index = jax.random.randint(ke, (2, N_EDGES), 0, N_NODES, dtype=jnp.int64)
        return {'x': x, 'edge_index': edge_index}
    _L2_gnn_all = _L2_gnn_setup()
    _L2_gnn_in = {k: v for k, v in _L2_gnn_all.items() if k in ()}
    del _L2_gnn_all

    def _L3_gnn_setup():
        import jax, jax.numpy as jnp
        import numpy as np
        N = 12500
        E = 200000
        ENC_EDGE = 32
        ENC_NODE = 64
        HIDDEN = 128
        key = jax.random.key(seed)
        ks = jax.random.split(key, 8)
        x = jax.random.normal(ks[0], (N, ENC_NODE), dtype=jnp.float32)
        edge_index = jax.random.randint(ks[1], (2, E), 0, N, dtype=jnp.int64)
        edge_attr = jax.random.normal(ks[2], (E, ENC_EDGE), dtype=jnp.float32)
        u = jax.random.normal(ks[3], (256, ENC_NODE), dtype=jnp.float32)
        batch = jax.random.randint(ks[4], (N,), 0, 256, dtype=jnp.int64)
        in1 = ENC_EDGE + ENC_NODE
        lim1 = float(np.sqrt(6.0 / (in1 + HIDDEN)))
        W1 = jax.random.uniform(ks[5], (in1, HIDDEN), minval=-lim1, maxval=lim1, dtype=jnp.float32)
        b1 = jnp.full((HIDDEN,), 0.01, dtype=jnp.float32)
        in2 = HIDDEN + ENC_NODE
        lim2 = float(np.sqrt(6.0 / (in2 + ENC_NODE)))
        W2 = jax.random.uniform(ks[6], (in2, ENC_NODE), minval=-lim2, maxval=lim2, dtype=jnp.float32)
        b2 = jnp.full((ENC_NODE,), 0.01, dtype=jnp.float32)
        return {'x': x, 'edge_index': edge_index, 'edge_attr': edge_attr, 'u': u, 'batch': batch, 'W1': W1, 'b1': b1, 'W2': W2, 'b2': b2}
    _L3_gnn_all = _L3_gnn_setup()
    _L3_gnn_in = {k: v for k, v in _L3_gnn_all.items() if k in ('u', 'W1', 'b1', 'W2', 'b2')}
    del _L3_gnn_all
    return {'x': x, 'src': src, 'dst': dst, 'edge_attr_16': edge_attr_16, 'edge_attr_32': edge_attr_32, 'L0_gnn_msg_w1': _L0_gnn_in['msg_w1'], 'L0_gnn_msg_b1': _L0_gnn_in['msg_b1'], 'L0_gnn_msg_w2': _L0_gnn_in['msg_w2'], 'L0_gnn_msg_b2': _L0_gnn_in['msg_b2'], 'L0_gnn_upd_w': _L0_gnn_in['upd_w'], 'L0_gnn_upd_b': _L0_gnn_in['upd_b'], 'L1_gnn_W_f': _L1_gnn_in['W_f'], 'L1_gnn_b_f': _L1_gnn_in['b_f'], 'L1_gnn_W_s': _L1_gnn_in['W_s'], 'L1_gnn_b_s': _L1_gnn_in['b_s'], 'L1_gnn_gamma': _L1_gnn_in['gamma'], 'L1_gnn_beta': _L1_gnn_in['beta'], 'L3_gnn_u': _L3_gnn_in['u'], 'L3_gnn_W1': _L3_gnn_in['W1'], 'L3_gnn_b1': _L3_gnn_in['b1'], 'L3_gnn_W2': _L3_gnn_in['W2'], 'L3_gnn_b2': _L3_gnn_in['b2']}

def reference(x, src, dst, edge_attr_16, edge_attr_32, L0_gnn_msg_w1, L0_gnn_msg_b1, L0_gnn_msg_w2, L0_gnn_msg_b2, L0_gnn_upd_w, L0_gnn_upd_b, L1_gnn_W_f, L1_gnn_b_f, L1_gnn_W_s, L1_gnn_b_s, L1_gnn_gamma, L1_gnn_beta, L3_gnn_u, L3_gnn_W1, L3_gnn_b1, L3_gnn_W2, L3_gnn_b2):
    import jax
    import jax.numpy as jnp

    def _L0_gnn_ref(node_features, edge_features, edge_index, msg_w1, msg_b1, msg_w2, msg_b2, upd_w, upd_b):
        import jax, jax.numpy as jnp
        import numpy as np
        N_NODES = 6250
        N_EDGES = 100000
        D_NODE = 64
        D_EDGE = 16
        D_HID = 64
        N_LAYERS = 3
        EPS = 1e-05

        def _ln(x):
            m = jnp.mean(x, axis=-1, keepdims=True)
            v = jnp.mean(jnp.square(x - m), axis=-1, keepdims=True)
            return (x - m) * jax.lax.rsqrt(v + EPS)

        def _ffn(x, w, b):
            return jax.nn.relu(_ln(x @ w + b))
        src = edge_index[0]
        dst = edge_index[1]
        x = node_features
        for l in range(N_LAYERS):
            m = jnp.concatenate([x[dst], x[src], edge_features], axis=-1)
            m = _ffn(m, msg_w1[l], msg_b1[l])
            m = _ffn(m, msg_w2[l], msg_b2[l])
            agg = jax.ops.segment_sum(m, dst, num_segments=N_NODES)
            h = jnp.concatenate([x, agg], axis=-1)
            x = x + _ffn(h, upd_w[l], upd_b[l])
        return x

    def _L1_gnn_ref(node_attrs, edge_index, edge_attrs, W_f, b_f, W_s, b_s, gamma, beta):
        import jax, jax.numpy as jnp
        import numpy as np
        N_NODES = 12500
        N_EDGES = 200000
        NODE_F = 64
        EDGE_F = 32
        BN_EPS = 1e-05
        source, target = (edge_index[0], edge_index[1])
        x_i = node_attrs[source]
        x_j = node_attrs[target]
        z = jnp.concatenate([x_i, x_j, edge_attrs], axis=-1)
        h = jax.nn.sigmoid(z @ W_f + b_f) * jax.nn.softplus(z @ W_s + b_s)
        message = jax.ops.segment_sum(h, source, num_segments=node_attrs.shape[0])
        mean = jnp.mean(message, axis=0)
        var = jnp.mean((message - mean) ** 2, axis=0)
        normed = (message - mean) * jax.lax.rsqrt(var + BN_EPS) * gamma + beta
        return node_attrs + normed

    def _L2_gnn_ref(x, edge_index):
        import jax, jax.numpy as jnp
        import numpy as np
        N_NODES = 12500
        N_EDGES = 156250
        D_FEAT = 64
        src, dst = (edge_index[0], edge_index[1])
        msgs = jnp.take(x, src, axis=0)
        out = jax.ops.segment_sum(msgs, dst, num_segments=x.shape[0])
        return out

    def _L3_gnn_ref(x, edge_index, edge_attr, u, batch, W1, b1, W2, b2):
        import jax, jax.numpy as jnp
        import numpy as np
        N = 12500
        E = 200000
        ENC_EDGE = 32
        ENC_NODE = 64
        HIDDEN = 128
        row, col = (edge_index[0], edge_index[1])
        msg = jnp.concatenate([x[row], edge_attr], axis=1)
        msg = msg @ W1 + b1
        agg = jax.ops.segment_sum(msg, col, num_segments=x.shape[0])
        out = jnp.concatenate([x, agg], axis=1)
        return out @ W2 + b2
    edge_index = jnp.stack([src, dst])
    batch0 = jnp.zeros((6250,), jnp.int32)
    h = jnp.maximum(_layernorm(x, axis=-1), 0.0)
    x = x + _L0_gnn_ref(h, edge_attr_16, edge_index, L0_gnn_msg_w1, L0_gnn_msg_b1, L0_gnn_msg_w2, L0_gnn_msg_b2, L0_gnn_upd_w, L0_gnn_upd_b)
    h = jnp.maximum(_layernorm(x, axis=-1), 0.0)
    x = x + _L1_gnn_ref(h, edge_index, edge_attr_32, L1_gnn_W_f, L1_gnn_b_f, L1_gnn_W_s, L1_gnn_b_s, L1_gnn_gamma, L1_gnn_beta)
    h = jnp.maximum(_layernorm(x, axis=-1), 0.0)
    x = x + _L2_gnn_ref(h, edge_index)
    h = jnp.maximum(_layernorm(x, axis=-1), 0.0)
    x = x + _L3_gnn_ref(h, edge_index, edge_attr_32, L3_gnn_u, batch0, L3_gnn_W1, L3_gnn_b1, L3_gnn_W2, L3_gnn_b2)
    return x

_drawn_inputs = setup_inputs


def setup_inputs(seed=0):
    import zlib

    import numpy as np

    out = dict(_drawn_inputs(seed))
    spreads = {'L0_gnn_msg_b1': (0.0, 0.1),
     'L0_gnn_msg_b2': (0.0, 0.1),
     'L0_gnn_upd_b': (0.0, 0.371),
     'L1_gnn_b_f': (0.0, 0.8),
     'L1_gnn_b_s': (0.0, 0.8),
     'L1_gnn_gamma': (1.0, 0.2),
     'L1_gnn_beta': (0.0, 0.1),
     'L3_gnn_b1': (0.009999999776482582, 0.6),
     'L3_gnn_b2': (0.009999999776482582, 0.6)}
    factors = {'edge_attr_16': 8.0}
    for name, (base, spread) in spreads.items():
        noise = np.random.default_rng([zlib.crc32(name.encode()), seed]).standard_normal(out[name].shape)
        drawn = base * np.exp(spread * noise) if base else spread * noise
        out[name] = jnp.asarray(drawn.astype(out[name].dtype))
    for name, factor in factors.items():
        out[name] = (out[name] * factor).astype(out[name].dtype)
    return out
```

```python
from contextlib import ExitStack, contextmanager

import concourse.bass as bass
from concourse import mybir

F32 = mybir.dt.float32
I32 = mybir.dt.int32
ALU = mybir.AluOpType
ACT = mybir.ActivationFunctionType
AX = mybir.AxisListType.X

P = 128
N = 6250
E = 200000
D = 64
E16, E32 = 16, 32
HID = 128
LAYERS = 3
EPS = 1e-5
NW = -(-N // P)
NPAD = NW * P
LASTW = N - (NW - 1) * P
GT = 4
GE = GT * P
NG = -(-E // GE) + NW
NG += -NG % 4
NS = NG * GE
NPAIR = NG // 4
NPAIR1 = NG // 2
CF = E // P
TAIL = E - P * CF
C = CF + (TAIL > 0)
CH = 11
assert CF % (2 * CH) == 0 and TAIL > 0
NCH = CF // CH // 2
RA = 52
RB = 34
A16, A32 = 2, 2 + E16
WC = 7
NWC = NW // WC
assert NW % WC == 0 and NG <= 4 * P
FILL = 110
assert (NS // P) % FILL == 0


def build(nc, x, src, dst, ea16, ea32, w1, b1, w2, b2, wu, bu, wf, bf, ws, bs, gamma, beta, v1, c1, v2, c2, out):
    ctx = ExitStack()

    def sb(name, shape, dt=F32):
        return ctx.enter_context(nc.sbuf_tensor(name, shape, dt))

    stage_sems = [[]]

    def sem(name):
        stage_sems[-1].append(nc.alloc_semaphore(name))
        return stage_sems[-1][-1]

    @contextmanager
    def new_stage():
        stage_sems.append([])
        yield
        nc.clear_and_free_semaphores(stage_sems.pop())
        nc.all_engine_barrier()

    def dram(name, shape, dt=F32):
        return nc.dram_tensor(name, shape, dt, kind="Internal").ap()

    with ctx:
        by_dst = dram("by_dst", [NS, RA])
        by_src = dram("by_src", [NS, RB])
        table = dram("table", [NPAD, D])
        table2 = dram("table2", [NPAD, 2 * D])
        window_row = [dram(f"window_row{k}", [1, 4 * P], I32) for k in range(2)]

        X = sb("X", [P, NW, D])
        H = sb("H", [P, NW, D])
        ACC = sb("ACC", [P, NW, D])
        NEAR = sb("NEAR", [P, NW, 2 * D])
        ACC2 = sb("ACC2", [P, NW, E32 + 1])
        node_ids = sb("node_ids", [P, NPAD])
        ident = sb("ident", [P, P])
        upper = sb("upper", [P, P])
        ones = sb("ones", [P, P])
        bins = sb("bins", [P, NW])
        valid = sb("valid", [P, 1])
        group_ids = sb("group_ids", [P, 4])
        window_of = sb("window_of", [1, 2, 4 * P], I32)

        wtab = sb("wtab", [D, LAYERS, 2 * D])
        wupd = sb("wupd", [2 * D, LAYERS, D])
        we = sb("we", [E16, LAYERS, D])
        wm2 = sb("wm2", [D, LAYERS, D])
        we_diag = sb("we_diag", [P, LAYERS, 8 * D])
        wm2_diag = sb("wm2_diag", [P, LAYERS, 2 * D])
        biases = sb("biases", [P, 3 * LAYERS, D])
        gate_bias = sb("gate_bias", [P, 2, D])
        gb = sb("gb", [P, 2, D])
        wgate = sb("wgate", [D, 4 * D])
        wge_diag = sb("wge_diag", [P, 4 * 2 * D])
        v1a = sb("v1a", [D, HID])
        v1b = sb("v1b", [E32 + 1, HID])
        v2a = sb("v2a", [D, D])
        v2b = sb("v2b", [HID, D])
        c2r = sb("c2r", [P, D])
        wmean = sb("wmean", [P, 5 * LAYERS + 1])
        bmean = sb("bmean", [P, 3 * LAYERS])

        stage = sb("stage", [P, WC, P])
        stage_t = sb("stage_t", [P, WC, P])
        far_rows = sb("far_rows", [P, WC, 2 * D])
        small = sb("small", [P, 4, NW])
        small_i = sb("small_i", [P, NW], I32)

        banks = [ctx.enter_context(nc.psum_tensor(f"bank{i}", [P, 512], F32)) for i in range(8)]

        turn = sem("turn")

        vector_step = sem("vector_step")
        vector_count = [0]

        def then(dve, ins):
            vector_count[0] += 1
            ins.then_inc(vector_step, 1)
            dve.wait_ge(vector_step, vector_count[0])

        weights_in = sem("weights_in")
        blocks_in = sem("blocks_in")
        iota_ready = sem("iota_ready")
        consts_ready = sem("consts_ready")
        zeroed = sem("zeroed")
        centred = sem("centred")
        pool_step = sem("pool_step")
        fill_ready = sem("fill_ready")
        filled = sem("filled")
        n_weights = [0]

        with ExitStack() as stack:
            ids_i = stack.enter_context(nc.sbuf_tensor("ids_i", [P, NPAD], I32))
            fill = stack.enter_context(nc.sbuf_tensor("fill", [P, FILL, RA], F32))
            block = stack.enter_context(nc.Block())

            @block.gpsimd
            def _(pool):
                pool.iota(ids_i[:], pattern=[[1, NPAD]], base=0, channel_multiplier=0).then_inc(iota_ready, 1)
                pool.memset(ident[:], 0.0).then_inc(pool_step, 1)
                pool.memset(upper[:], 1.0).then_inc(pool_step, 1)
                pool.memset(ones[:], 1.0).then_inc(pool_step, 1)
                pool.iota(group_ids[:].bitcast(I32), pattern=[[1, 4]], base=0, channel_multiplier=4).then_inc(iota_ready, 1)
                pool.memset(valid[:], 1.0).then_inc(pool_step, 1)
                pool.wait_ge(pool_step, 4)
                pool.affine_select(out=ident[:], in_=ident[:], compare_op=ALU.not_equal, fill=1.0, base=0,
                                   pattern=[[-1, P]], channel_multiplier=1).then_inc(consts_ready, 1)
                pool.affine_select(out=upper[:], in_=upper[:], compare_op=ALU.is_ge, fill=0.0, base=-1,
                                   pattern=[[1, P]], channel_multiplier=-1).then_inc(consts_ready, 1)
                pool.affine_select(out=valid[:], in_=valid[:], compare_op=ALU.is_ge, fill=0.0, base=LASTW - 1,
                                   pattern=[[0, 1]], channel_multiplier=-1).then_inc(consts_ready, 1)
                pool.wait_ge(consts_ready, 3)

            @block.sync
            def _(sp):
                def load(to, frm):
                    n_weights[0] += 16
                    sp.dma_start(to, frm).then_inc(weights_in, 16)

                def load_late(to, frm):
                    sp.dma_start(to, frm).then_inc(blocks_in, 16)

                def spread(v):
                    return v.rearrange("(a n) -> a n", a=1).broadcast_to([P, v.shape[0]])

                for l in range(LAYERS):
                    load(wtab[:, l, 0:D], w1[l, 0:D, :])
                    load(wtab[:, l, D:], w1[l, D:2 * D, :])
                    load(we[:, l, :], w1[l, 2 * D:, :])
                    load(wm2[:, l, :], w2[l])
                    load(wupd[:, l, :], wu[l])
                    load(biases[:, l, :], spread(b1[l]))
                    load(biases[:, LAYERS + l, :], spread(b2[l]))
                    load(biases[:, 2 * LAYERS + l, :], spread(bu[l]))
                for k, (w, b) in enumerate(((wf, bf), (ws, bs))):
                    load(wgate[:, k * D:(k + 1) * D], w[0:D, :])
                    load(wgate[:, (2 + k) * D:(3 + k) * D], w[D:2 * D, :])
                    load(gate_bias[:, k, :], spread(b))
                load(gb[:, 0, :], spread(gamma))
                load(gb[:, 1, :], spread(beta))
                load(v1a[:], v1[0:D, :])
                load(v1b[0:E32, :], v1[D:, :])
                load(v1b[E32:E32 + 1, :], c1.rearrange("(a n) -> a n", a=1))
                load(v2a[:], v2[0:D, :])
                load(v2b[:], v2[D:, :])
                load(c2r[:], spread(c2))
                sp.wait_ge(zeroed, 3)
                load_late(X[:, 0:NW - 1, :], x[0:(NW - 1) * P, :].rearrange("(w p) f -> p w f", p=P))
                load_late(X[0:LASTW, NW - 1, :], x[(NW - 1) * P:, :])
                for t in range(4):
                    for k, w in enumerate((wf, ws)):
                        load_late(wge_diag[E32 * t:E32 * (t + 1), (2 * t + k) * D:(2 * t + k + 1) * D], w[2 * D:, :])
                sp.wait_ge(centred, 1)
                for l in range(LAYERS):
                    for t in range(8):
                        sp.dma_start(we_diag[E16 * t:E16 * (t + 1), l, D * t:D * (t + 1)],
                                     we[:, l, :]).then_inc(blocks_in, 16)
                    for t in range(2):
                        sp.dma_start(wm2_diag[D * t:D * (t + 1), l, D * t:D * (t + 1)],
                                     wm2[:, l, :]).then_inc(blocks_in, 16)
                sp.wait_ge(blocks_in, 16 * (10 * LAYERS + 10))
                assert n_weights[0] == 16 * (8 * LAYERS + 14), n_weights

            @block.scalar
            def _(act):
                act.wait_ge(fill_ready, 1)
                rows = NS // P
                for k in range(rows // FILL):
                    act.dma_start(by_dst.rearrange("(p r) f -> p r f", p=P)[:, k * FILL:(k + 1) * FILL, :],
                                  fill[:]).then_inc(filled, 16)
                act.wait_ge(filled, 16 * (rows // FILL))
                act.wait_ge(fill_ready, 2)
                flat = fill[:].rearrange("p r f -> p (r f)")[:, 0:FILL * RB]
                for k in range(rows // FILL):
                    act.dma_start(by_src.rearrange("(p r) f -> p (r f)", p=P)[:, k * FILL * RB:(k + 1) * FILL * RB],
                                  flat).then_inc(filled, 16)
                act.wait_ge(filled, 32 * (rows // FILL))

            @block.vector
            def _(dve):
                dve.memset(X[:], 0.0).then_inc(zeroed, 1)
                dve.memset(we_diag[:], 0.0)
                dve.memset(wm2_diag[:], 0.0).then_inc(zeroed, 1)
                dve.memset(wge_diag[:], 0.0).then_inc(zeroed, 1)
                dve.memset(stage[:], 0.0)
                then(dve, dve.memset(fill[:], 0.0))
                dve.memset(fill[:, :, 0:1], -1.0).then_inc(fill_ready, 1)
                dve.wait_ge(iota_ready, 2)
                dve.tensor_copy(node_ids[:], ids_i[:])
                dve.tensor_copy(bins[:], ids_i[:, 0:NW])
                then(dve, dve.tensor_copy(small[:, 0, 0:4], group_ids[:].bitcast(I32)))
                then(dve, dve.tensor_copy(group_ids[:], small[:, 0, 0:4]))
                dve.wait_ge(weights_in, 16 * (8 * LAYERS + 14))
                mats = []
                for l in range(LAYERS):
                    mats += [wtab[:, l, 0:D], wtab[:, l, D:], we[:, l, :], wm2[:, l, :], wupd[:, l, :]]
                for k, m in enumerate(mats):
                    last = dve.tensor_reduce(wmean[0:m.shape[0], k:k + 1], m, AX, ALU.add)
                then(dve, dve.tensor_reduce(bmean[:], biases[:], AX, ALU.add))
                for k, m in enumerate(mats):
                    r = m.shape[0]
                    then(dve, dve.tensor_scalar(wmean[0:r, k:k + 1], wmean[0:r, k:k + 1], 1.0 / D, None, ALU.mult))
                    last = dve.tensor_scalar(m, m, wmean[0:r, k:k + 1], None, ALU.subtract)
                then(dve, last)
                then(dve, dve.tensor_scalar(bmean[:], bmean[:], 1.0 / D, None, ALU.mult))
                dve.tensor_tensor(biases[:], biases[:], bmean[:].rearrange("p (k a) -> p k a", a=1).broadcast_to(
                    [P, 3 * LAYERS, D]), ALU.subtract).then_inc(centred, 1)
                dve.wait_ge(filled, 16 * (NS // P // FILL))
                flat = fill[:].rearrange("p r f -> p (r f)")[:, 0:FILL * RB]
                then(dve, dve.memset(flat, 0.0))
                dve.memset(flat.rearrange("p (r f) -> p r f", f=RB)[:, :, 0:1], -1.0).then_inc(fill_ready, 1)

        order = ExitStack()
        keys_i = [order.enter_context(nc.sbuf_tensor(f"keys_i{k}", [P, C], I32)) for k in range(2)]
        key_f = order.enter_context(nc.sbuf_tensor("key_f", [P, C], F32))
        win_f = order.enter_context(nc.sbuf_tensor("win_f", [P, C], F32))
        mask = order.enter_context(nc.sbuf_tensor("mask", [P, C], I32))
        run = order.enter_context(nc.sbuf_tensor("run", [P, C], F32))
        place_f = order.enter_context(nc.sbuf_tensor("place_f", [P, C], F32))
        place = [order.enter_context(nc.sbuf_tensor(f"place{k}", [P, C], I32)) for k in range(2)]
        hist = order.enter_context(nc.sbuf_tensor("hist", [P, NW], F32))
        ends = order.enter_context(nc.sbuf_tensor("ends", [P, NW], F32))
        before = order.enter_context(nc.sbuf_tensor("before", [P, 4, NW], F32))
        win4 = order.enter_context(nc.sbuf_tensor("win4", [P, 4], F32))
        win4_i = order.enter_context(nc.sbuf_tensor("win4_i", [P, 4], I32))
        st16 = [order.enter_context(nc.sbuf_tensor(f"st16_{k}", [P, CH, E16], F32)) for k in range(2)]
        st32 = [order.enter_context(nc.sbuf_tensor(f"st32_{k}", [P, CH, E32], F32)) for k in range(2)]
        recs = [order.enter_context(nc.sbuf_tensor(f"recs{k}", [P, CH, RA], F32)) for k in range(2)]
        slots = [order.enter_context(nc.sbuf_tensor(f"slots{k}", [P, CH], I32)) for k in range(2)]

        keys_in = sem("keys_in")
        keys_loaded = sem("keys_loaded")
        windows_out = [sem(f"windows_out{k}") for k in range(2)]
        hist_ready = [sem(f"hist_ready{k}") for k in range(2)]
        hist_ps = [sem(f"hist_ps{k}") for k in range(2)]
        win4_ready = [sem(f"win4_ready{k}") for k in range(2)]
        mask_ready = [sem(f"mask_ready{k}") for k in range(2)]
        run_ready = [sem(f"run_ready{k}") for k in range(2)]
        picked = [sem(f"picked{k}") for k in range(2)]
        counts_ps, prefix_ps = banks[0][:, 0:NW], banks[1][:, 0:NW]

        def rank_vector(dve, k):
            then(dve, dve.tensor_copy(win_f[:], keys_i[k][:]))
            then(dve, dve.tensor_scalar(mask[:], keys_i[k][:], 7, None, ALU.arith_shift_right))
            then(dve, dve.tensor_copy(win_f[:], mask[:]))
            then(dve, dve.memset(place_f[:], 1.0))
            with dve.Fori(0, NW) as b:
                dve.tensor_scalar(run[:], win_f[:], bins[:, bass.ds(b, 1)], None, ALU.is_equal, ALU.add,
                                  accum_out=hist[:, bass.ds(b, 1)]).then_inc(hist_ready[k], 1)
                dve.wait_ge(hist_ready[k], b + 1)
            dve.wait_ge(hist_ps[k], 1)
            groups, start, low, cum = small[:, 0, :], small[:, 1, :], small[:, 2, :], small[:, 3, :]
            then(dve, dve.tensor_scalar(low, counts_ps, float(GE - 1), None, ALU.add))
            then(dve, dve.tensor_copy(small_i[:], low))
            then(dve, dve.tensor_scalar(small_i[:], small_i[:], 9, None, ALU.arith_shift_right))
            then(dve, dve.tensor_copy(groups, small_i[:]))
            then(dve, dve.tensor_tensor_scan(ends[:], groups, groups, 0.0, ALU.add, ALU.max))
            then(dve, dve.tensor_tensor(start, ends[:], groups, ALU.subtract))
            then(dve, dve.scalar_tensor_tensor(out=cum, in0=start, scalar=float(GE), in1=prefix_ps,
                                               op0=ALU.mult, op1=ALU.add))
            then(dve, dve.tensor_tensor(before[:], ends[:].rearrange("p (a w) -> p a w", a=1).broadcast_to([P, 4, NW]),
                                        group_ids[:].rearrange("p (g a) -> p g a", a=1).broadcast_to([P, 4, NW]),
                                        ALU.is_le))
            then(dve, dve.tensor_reduce(win4[:], before[:], AX, ALU.add))
            then(dve, dve.tensor_scalar(win4[:], win4[:], float(NW - 1), None, ALU.min))
            dve.tensor_copy(win4_i[:], win4[:]).then_inc(win4_ready[k], 1)
            with dve.Fori(0, NW) as b:
                n = b + 1
                dve.tensor_scalar(mask[:], win_f[:], bins[:, bass.ds(b, 1)], None,
                                  ALU.is_equal).then_inc(mask_ready[k], 1)
                dve.wait_ge(mask_ready[k], n)
                dve.tensor_tensor_scan(run[:], mask[:], mask[:], cum_of(b), ALU.add, ALU.max).then_inc(run_ready[k], 1)
                dve.wait_ge(run_ready[k], n)
                dve.sem_inc(turn, 1)
                dve.copy_predicated(place_f[:], mask[:], run[:]).then_inc(picked[k], 1)
                dve.wait_ge(picked[k], n)
            then(dve, dve.tensor_scalar(place[k][:], place_f[:], -1.0, None, ALU.add))

        def cum_of(b):
            return small[:, 3, bass.ds(b, 1)]

        def rank_tensor(pe, k):
            pe.wait_ge(hist_ready[k], NW)
            pe.matmul(counts_ps, lhsT=ones[:], rhs=hist[:], start=True, stop=True)
            pe.matmul(prefix_ps, lhsT=upper[:], rhs=hist[:], start=True, stop=True).then_inc(hist_ps[k], 1)

        def rank_windows(sp, k):
            sp.wait_ge(win4_ready[k], 1)
            sp.dma_start(window_row[k].rearrange("a (p c) -> (a p) c", p=P), win4_i[:]).then_inc(windows_out[k], 16)
            sp.wait_ge(windows_out[k], 16)
            sp.dma_start(window_of[:, k, :], window_row[k]).then_inc(windows_out[k], 16)
            sp.wait_ge(windows_out[k], 32)

        with nc.Block() as block:
            @block.sync
            def _(sp):
                sp.wait_ge(keys_in, 1)
                for keys, to in ((dst, keys_i[0]), (src, keys_i[1])):
                    sp.dma_start(to[:, 0:CF], keys[0:P * CF].rearrange("(p c) -> p c", p=P)).then_inc(keys_loaded, 16)
                    sp.dma_start(to[0:TAIL, CF:C], keys[P * CF:].rearrange("(p c) -> p c", c=1)).then_inc(keys_loaded, 16)
                sp.wait_ge(keys_loaded, 64)
                rank_windows(sp, 0)

            @block.vector
            def _(dve):
                then(dve, dve.memset(keys_i[0][:, CF:C], NPAD))
                dve.memset(keys_i[1][:, CF:C], NPAD).then_inc(keys_in, 1)
                dve.wait_ge(keys_loaded, 64)
                rank_vector(dve, 0)

            @block.tensor
            def _(pe):
                rank_tensor(pe, 0)

        def scatter(k):
            width, target, a32 = ((RA, by_dst, A32), (RB, by_src, 2))[k]
            staged = [sem(f"staged{k}_{i}") for i in range(2)]
            rec_ready = [sem(f"rec_ready{k}_{i}") for i in range(2)]
            scattered = [sem(f"scattered{k}_{i}") for i in range(2)]
            tail_done = sem(f"tail_done{k}")
            act_step = sem(f"rec_step{k}")
            e16_c = ea16[0:P * CF, :].rearrange("(p c) f -> p c f", p=P)
            e32_c = ea32[0:P * CF, :].rearrange("(p c) f -> p c f", p=P)
            loads = 1 if k else 2
            copies = 5 - k
            rec = [r[:].rearrange("p c f -> p (c f)")[:, 0:CH * width].rearrange("p (c f) -> p c f", f=width)
                   for r in recs]

            with nc.Block() as block:
                @block.sync
                def _(sp):
                    def load(h, i, first):
                        if not first:
                            sp.wait_ge(rec_ready[h], i * copies)
                        cols = bass.ds((2 * i + h) * CH, CH)
                        if k == 0:
                            sp.dma_start(st16[h][:], e16_c[:, cols, :]).then_inc(staged[h], 16)
                        sp.dma_start(st32[h][:], e32_c[:, cols, :]).then_inc(staged[h], 16)

                    load(0, 0, True)
                    load(1, 0, True)
                    with sp.Fori(1, NCH) as i:
                        load(0, i, False)
                        load(1, i, False)
                    sp.wait_ge(rec_ready[0], NCH * copies)
                    if k == 0:
                        sp.dma_start(st16[0][0:TAIL, 0, :], ea16[P * CF:, :]).then_inc(staged[0], 16)
                    sp.dma_start(st32[0][0:TAIL, 0, :], ea32[P * CF:, :]).then_inc(staged[0], 16)
                    if k == 0:
                        rank_windows(sp, 1)

                @block.scalar
                def _(act):
                    if k == 0:
                        for r in rec:
                            act.activation(r[:, :, RA - 2], ones[:, 0:CH], ACT.Copy)
                            act.activation(r[:, :, RA - 1], ones[:, 0:CH], ACT.Copy, scale=0.0).then_inc(act_step, 1)
                    act.activation(key_f[:], keys_i[k][:], ACT.Copy).then_inc(act_step, 1)
                    act.wait_ge(act_step, 3 if k == 0 else 1)

                    def records(h, n, lanes, cols, count, i=None):
                        act.wait_ge(staged[h], 16 * loads * n)
                        if i is not None:
                            act.wait_ge(scattered[h], 16 * CH * i)
                        if k == 0:
                            act.activation(rec[h][0:lanes, 0:count, A16:A16 + E16], st16[h][0:lanes, 0:count, :],
                                           ACT.Copy).then_inc(rec_ready[h], 1)
                        act.activation(rec[h][0:lanes, 0:count, a32:a32 + E32], st32[h][0:lanes, 0:count, :],
                                       ACT.Copy).then_inc(rec_ready[h], 1)
                        act.activation(rec[h][0:lanes, 0:count, 0], key_f[0:lanes, cols],
                                       ACT.Copy).then_inc(rec_ready[h], 1)
                        act.activation(rec[h][0:lanes, 0:count, 1].bitcast(I32), keys_i[1 - k][0:lanes, cols],
                                       ACT.Copy).then_inc(rec_ready[h], 1)
                        act.activation(slots[h][0:lanes, 0:count], place[k][0:lanes, cols],
                                       ACT.Copy).then_inc(rec_ready[h], 1)

                    for h in range(2):
                        records(h, 1, P, bass.ds(h * CH, CH), CH)
                    with act.Fori(1, NCH) as i:
                        for h in range(2):
                            records(h, i + 1, P, bass.ds((2 * i + h) * CH, CH), CH, i)
                    records(0, NCH + 1, TAIL, slice(CF, C), 1, NCH)

                @block.gpsimd
                def _(pool):
                    def write(h, n):
                        pool.wait_ge(rec_ready[h], copies * n)
                        pool.sem_inc(turn, 1)
                        for j in range(CH):
                            pool.indirect_dma_start(
                                out=target, out_offset=bass.IndirectOffsetOnAxis(ap=slots[h][:, j:j + 1], axis=0),
                                in_=rec[h][:, j, :], in_offset=None).then_inc(scattered[h], 16)

                    with pool.Fori(0, NCH) as i:
                        write(0, i + 1)
                        write(1, i + 1)
                    pool.wait_ge(rec_ready[0], copies * (NCH + 1))
                    pool.indirect_dma_start(
                        out=target, out_offset=bass.IndirectOffsetOnAxis(ap=slots[0][0:TAIL, 0:1], axis=0),
                        in_=rec[0][0:TAIL, 0, :], in_offset=None).then_inc(tail_done, 16)
                    pool.wait_ge(scattered[0], 16 * CH * NCH)
                    pool.wait_ge(scattered[1], 16 * CH * NCH)
                    pool.wait_ge(tail_done, 16)

                if k == 0:
                    @block.vector
                    def _(dve):
                        rank_vector(dve, 1)

                    @block.tensor
                    def _(pe):
                        rank_tensor(pe, 1)

        with new_stage():
            scatter(0)
        with new_stage():
            scatter(1)
        order.close()

        sqrt_done = sem("sqrt_done")
        sqrt_asked = sem("sqrt_asked")
        n_sqrt = [0]
        S = NEAR[:, :, 0:D]
        mean, rstd = small[:, 0, :], small[:, 1, :]

        def wide(v):
            return v.rearrange("p (w a) -> p w a", a=1).broadcast_to([P, NW, D])

        def over(v):
            return v.rearrange("p (a f) -> p a f", a=1).broadcast_to([P, NW, D])

        def norm_relu(dve, to, frm):
            then(dve, dve.tensor_reduce(mean, frm, AX, ALU.add))
            then(dve, dve.tensor_scalar(mean, mean, 1.0 / D, None, ALU.mult))
            then(dve, dve.tensor_tensor(to, frm, wide(mean), ALU.subtract))
            then(dve, dve.tensor_tensor(S, to, to, ALU.mult))
            then(dve, dve.tensor_reduce(rstd, S, AX, ALU.add))
            then(dve, dve.tensor_scalar(rstd, rstd, 1.0 / D, EPS, ALU.mult, ALU.add))
            root(dve, rstd)
            then(dve, dve.reciprocal(rstd, rstd))
            then(dve, dve.scalar_tensor_tensor(out=to, in0=to, scalar=0.0, in1=wide(rstd), op0=ALU.max, op1=ALU.mult))

        roots = []

        def root(dve, v):
            n_sqrt[0] += 1
            roots.append((v, n_sqrt[0]))
            dve.sem_inc(sqrt_asked, 1)
            dve.wait_ge(sqrt_done, n_sqrt[0])

        def take_roots(act):
            for v, n in roots:
                act.wait_ge(sqrt_asked, n)
                act.activation(v, v, ACT.Sqrt).then_inc(sqrt_done, 1)
            roots.clear()

        def node_block(steps):
            with nc.Block() as block:
                @block.vector
                def _(dve):
                    steps(dve)

                @block.scalar
                def _(act):
                    take_roots(act)

        def linear(name, weight, width, k_rows, near, near_width, far=None):
            staged, turned = sem(name + "_staged"), sem(name + "_turned")
            turned_in, product, taken = sem(name + "_turned_in"), sem(name + "_product"), sem(name + "_taken")
            far_ready, far_out = sem(name + "_far_ready"), sem(name + "_far_out")
            per = 512 // width
            parts = [(a, min(a + per, WC)) for a in range(0, WC, per)]
            halves = [(0, 4), (4, WC)]
            far_width = width - near_width
            both = 2 if k_rows == P else 1

            with nc.Block() as block:
                @block.vector
                def _(dve):
                    def put(i, n, first):
                        if not first:
                            dve.wait_ge(turned, i)
                        dve.tensor_copy(stage[:, :, 0:D], H[:, bass.ds(i * WC, WC), :]).then_inc(staged, 1)
                        if both == 2:
                            dve.tensor_copy(stage[:, :, D:], ACC[:, bass.ds(i * WC, WC), :]).then_inc(staged, 1)

                    put(0, 1, True)
                    with dve.Fori(1, NWC) as i:
                        put(i, i + 1, False)

                @block.tensor
                def _(pe):
                    def go(n):
                        pe.wait_ge(staged, n * both)
                        for j in range(WC):
                            last = pe.transpose(banks[j // 4][:, (j % 4) * P:(j % 4 + 1) * P], stage[:, j, :], ident[:])
                        last.then_inc(turned, 1)
                        pe.wait_ge(turned_in, 2 * n)
                        for q, (a, b) in enumerate(parts):
                            for j in range(a, b):
                                last = pe.matmul(banks[2 + q][:, (j - a) * width:(j - a + 1) * width],
                                                 lhsT=stage_t[0:k_rows, j, :], rhs=weight, start=True, stop=True)
                        last.then_inc(product, 1)

                    go(1)
                    with pe.Fori(1, NWC) as i:
                        pe.wait_ge(taken, i)
                        go(i + 1)

                @block.scalar
                def _(act):
                    def go(i, n, first):
                        act.wait_ge(turned, n)
                        for q, (a, b) in enumerate(halves):
                            act.activation(stage_t[:, a:b, :].rearrange("p j f -> p (j f)"),
                                           banks[q][:, 0:(b - a) * P], ACT.Copy).then_inc(turned_in, 1)
                        act.wait_ge(product, n)
                        if far is not None and not first:
                            act.wait_ge(far_out, 16 * i)
                        for q, (a, b) in enumerate(parts):
                            rows = banks[2 + q][:, 0:(b - a) * width].rearrange("p (j f) -> p j f", f=width)
                            last = act.activation(near[:, bass.ds(i * WC + a, b - a), 0:near_width],
                                                  rows[:, :, 0:near_width], ACT.Copy)
                            if far is not None:
                                act.activation(far_rows[:, a:b, 0:far_width], rows[:, :, near_width:],
                                               ACT.Copy).then_inc(far_ready, 1)
                        act.activation(act_mark[:], ones[:, 0:1], ACT.Copy).then_inc(taken, 1)

                    go(0, 1, True)
                    with act.Fori(1, NWC) as i:
                        go(i, i + 1, False)

                if far is not None:
                    @block.sync
                    def _(sp):
                        rows = far.rearrange("(w p) f -> p w f", p=P)
                        with sp.Fori(0, NWC) as i:
                            sp.wait_ge(far_ready, (i + 1) * len(parts))
                            sp.dma_start(rows[:, bass.ds(i * WC, WC), :],
                                         far_rows[:, :, 0:far_width]).then_inc(far_out, 16)
                        sp.wait_ge(far_out, 16 * NWC)

        act_mark = sb("act_mark", [P, 1])

        edge = ctx.enter_context(ExitStack())

        def eb(name, shape, dt=F32):
            return [edge.enter_context(nc.sbuf_tensor(f"{name}{h}", shape, dt)) for h in range(2)]

        rec = eb("rec", [P, 2, GT, RA])
        far_in = eb("far_in", [P, 2 * GT, D])
        onehot = eb("onehot", [P, 2 * GT, P])
        onehot_t = eb("onehot_t", [P, 2 * GT, P])
        e_flat = eb("e_flat", [P, P])
        e_t = eb("e_t", [P, P])
        z = eb("z", [P, 2 * GT, D])
        zz = eb("zz", [P, 2 * GT, D])
        zr = eb("zr", [P, 2 * GT, D])
        zr_t = eb("zr_t", [P, GT, P])
        biased = eb("biased", [P, 2 * GT, D])
        stat = eb("stat", [P, 6, 2 * GT])

        slot_rows = {0: by_dst.rearrange("(g p j) f -> p g (j f)", p=P, j=GT),
                     1: by_src.rearrange("(g p j) f -> p g (j f)", p=P, j=GT)}

        def per_tile(v, n, width):
            return v.rearrange("p (t a) -> p t a", a=1).broadcast_to([P, n, width])

        def equal_nodes(dve, to, w, near_keys):
            ids = node_ids[:, bass.ds(w * P, P)].rearrange("p (a n) -> p a n", a=1).broadcast_to([P, GT, P])
            return dve.tensor_tensor(to, ids, near_keys.broadcast_to([P, GT, P]), ALU.is_equal)

        mpnn_names = ("rec_in", "far_ready", "e_ready", "onehot_ready", "turned", "turned_sb", "h_ps", "z_ready",
                 "square1", "sum1", "var1", "root1", "relu_ready", "relu_turned", "relu_t", "v_ps", "bias_ready",
                 "v_ready", "square2", "sum2", "epsvar", "var2", "root2", "rec2", "m_ready", "acc_ps", "acc_added", "acc_mid")
        def mpnn_pass(l):
            s = {n: [sem(f"{n}{h}_l{l}") for h in range(2)] for n in mpnn_names}
            rows = slot_rows[0]

            with nc.Block() as block:
                @block.sync
                def _(sp):
                    def load(h, i, first):
                        if not first:
                            sp.wait_ge(s["onehot_ready"][h], 2 * i)
                            sp.wait_ge(s["e_ready"][h], i)
                            sp.wait_ge(s["z_ready"][h], i)
                        sp.dma_start(rec[h][:].rearrange("p g j f -> p g (j f)"),
                                     rows[:, bass.ds(4 * i + 2 * h, 2), :]).then_inc(s["rec_in"][h], 16)

                    for h in range(2):
                        load(h, 0, True)
                    with sp.Fori(1, NPAIR) as i:
                        for h in range(2):
                            load(h, i, False)

                @block.gpsimd
                def _(pool):
                    def gather(h, i, first):
                        pool.wait_ge(s["rec_in"][h], 16 * (i + 1))
                        if not first:
                            pool.wait_ge(s["z_ready"][h], i)
                        pool.sem_inc(turn, 1)
                        for t in range(2 * GT):
                            pool.indirect_dma_start(
                                out=far_in[h][:, t, :], out_offset=None, in_=table,
                                in_offset=bass.IndirectOffsetOnAxis(
                                    ap=rec[h][:, t // GT, t % GT, 1:2].bitcast(I32), axis=0),
                            ).then_inc(s["far_ready"][h], 16)

                    for h in range(2):
                        gather(h, 0, True)
                    with pool.Fori(1, NPAIR) as i:
                        for h in range(2):
                            gather(h, i, False)

                @block.vector
                def _(dve):
                    def step(h, i):
                        n = i + 1
                        st = stat[h]
                        dve.wait_ge(s["rec_in"][h], 16 * (i + 1))
                        w = [dve.value_load(window_of[0:1, 0, bass.ds(4 * i + 2 * h + g, 1)], min_val=0, max_val=NW - 1)
                             for g in range(2)]
                        for g in range(2):
                            equal_nodes(dve, onehot[h][:, g * GT:(g + 1) * GT, :], w[g],
                                        rec[h][:, g, :, 0:1]).then_inc(s["onehot_ready"][h], 1)
                        dve.wait_ge(s["far_ready"][h], 128 * (i + 1))
                        dve.wait_ge(s["h_ps"][h], n)
                        flat = z[h][:].rearrange("p t f -> p (t f)")
                        dve.tensor_tensor(flat, banks[4 * h + 3][:], far_in[h][:].rearrange("p t f -> p (t f)"),
                                          ALU.add).then_inc(s["z_ready"][h], 1)
                        dve.wait_ge(s["square1"][h], n)
                        dve.tensor_reduce(st[:, 0, :], zz[h][:], AX, ALU.add).then_inc(s["sum1"][h], 1)
                        dve.wait_ge(s["sum1"][h], n)
                        dve.tensor_scalar(st[:, 1, :], st[:, 0, :], 1.0 / D, EPS, ALU.mult,
                                          ALU.add).then_inc(s["var1"][h], 1)
                        dve.wait_ge(s["var1"][h], n)
                        dve.wait_ge(s["root1"][h], n)
                        dve.tensor_tensor(biased[h][:], per_tile(st[:, 2, :], 2 * GT, D),
                                          biases[:, LAYERS + l:LAYERS + l + 1, :].broadcast_to([P, 2 * GT, D]),
                                          ALU.mult).then_inc(s["bias_ready"][h], 1)
                        dve.tensor_scalar(st[:, 3, :], st[:, 1, :], EPS, None, ALU.mult).then_inc(s["epsvar"][h], 1)
                        dve.wait_ge(s["bias_ready"][h], n)
                        dve.wait_ge(s["v_ps"][h], n)
                        dve.tensor_tensor(flat, banks[4 * h + 1][:], biased[h][:].rearrange("p t f -> p (t f)"),
                                          ALU.add).then_inc(s["v_ready"][h], 1)
                        dve.wait_ge(s["epsvar"][h], n)
                        dve.wait_ge(s["square2"][h], n)
                        dve.tensor_reduce(st[:, 0, :], zz[h][:], AX, ALU.add).then_inc(s["sum2"][h], 1)
                        dve.wait_ge(s["sum2"][h], n)
                        dve.scalar_tensor_tensor(out=st[:, 4, :], in0=st[:, 0, :], scalar=1.0 / D, in1=st[:, 3, :],
                                                 op0=ALU.mult, op1=ALU.add).then_inc(s["var2"][h], 1)
                        dve.wait_ge(s["root2"][h], n)
                        dve.reciprocal(st[:, 5, :], st[:, 4, :]).then_inc(s["rec2"][h], 1)
                        dve.wait_ge(s["rec2"][h], n)
                        dve.scalar_tensor_tensor(out=z[h][:], in0=z[h][:], scalar=0.0, in1=per_tile(st[:, 5, :], 2 * GT, D),
                                                 op0=ALU.max, op1=ALU.mult).then_inc(s["m_ready"][h], 1)
                        dve.wait_ge(s["acc_ps"][h], n)
                        for g in range(2):
                            row = ACC[:, bass.ds(w[g], 1), :].rearrange("p a f -> p (a f)")
                            mark = s["acc_added" if g else "acc_mid"][h]
                            dve.tensor_tensor(row, row, banks[4 * h + 2][:, g * D:(g + 1) * D], ALU.add).then_inc(mark, 1)
                            dve.wait_ge(mark, n)

                    with dve.Fori(0, NPAIR) as i:
                        for h in range(2):
                            step(h, i)

                @block.scalar
                def _(act):
                    def step(h, i):
                        n = i + 1
                        st = stat[h]
                        b0, b1_, b2_, _ = banks[4 * h:4 * h + 4]
                        act.wait_ge(s["rec_in"][h], 16 * (i + 1))
                        act.activation(e_flat[h][:].rearrange("p (g j f) -> p (g j) f", g=2, j=GT),
                                       rec[h][:, :, :, A16:A16 + E16].rearrange("p g j f -> p (g j) f"),
                                       ACT.Copy).then_inc(s["e_ready"][h], 1)
                        act.wait_ge(s["turned"][h], n)
                        act.activation(onehot_t[h][:, 0:GT, :].rearrange("p t f -> p (t f)"), b0[:], ACT.Copy)
                        act.activation(onehot_t[h][:, GT:, :].rearrange("p t f -> p (t f)"), b1_[:], ACT.Copy)
                        act.activation(e_t[h][:], b2_[:, 0:P], ACT.Copy).then_inc(s["turned_sb"][h], 1)
                        act.wait_ge(s["z_ready"][h], n)
                        act.activation(zz[h][:], z[h][:], ACT.Square).then_inc(s["square1"][h], 1)
                        act.activation(zr[h][:], z[h][:], ACT.Relu).then_inc(s["relu_ready"][h], 1)
                        act.wait_ge(s["var1"][h], n)
                        act.activation(st[:, 2, :], st[:, 1, :], ACT.Sqrt).then_inc(s["root1"][h], 1)
                        act.wait_ge(s["relu_turned"][h], n)
                        act.activation(zr_t[h][:].rearrange("p t f -> p (t f)"), b0[:], ACT.Copy).then_inc(s["relu_t"][h], 1)
                        act.wait_ge(s["v_ready"][h], n)
                        act.activation(zz[h][:], z[h][:], ACT.Square).then_inc(s["square2"][h], 1)
                        act.wait_ge(s["var2"][h], n)
                        act.activation(st[:, 4, :], st[:, 4, :], ACT.Sqrt).then_inc(s["root2"][h], 1)

                    with act.Fori(0, NPAIR) as i:
                        for h in range(2):
                            step(h, i)

                @block.tensor
                def _(pe):
                    def step(h, i):
                        n = i + 1
                        b0, b1_, b2_, b3 = banks[4 * h:4 * h + 4]
                        w = [pe.value_load(window_of[0:1, 0, bass.ds(4 * i + 2 * h + g, 1)], min_val=0, max_val=NW - 1)
                             for g in range(2)]
                        pe.wait_ge(s["e_ready"][h], n)
                        pe.transpose(b2_[:, 0:P], e_flat[h][:], ident[:])
                        for t in range(2 * GT):
                            if t % GT == 0:
                                pe.wait_ge(s["onehot_ready"][h], 2 * n - 1 + t // GT)
                            bank = b1_ if t >= GT else b0
                            last = pe.transpose(bank[:, (t % GT) * P:(t % GT + 1) * P], onehot[h][:, t, :], ident[:])
                        last.then_inc(s["turned"][h], 1)
                        pe.wait_ge(s["turned_sb"][h], n)
                        pe.matmul(b3[:], lhsT=e_t[h][:], rhs=we_diag[:, l, :], start=True, stop=False,
                                  skip_group_check=True)
                        for t in range(2 * GT):
                            last = pe.matmul(b3[:, t * D:(t + 1) * D], lhsT=onehot_t[h][:, t, :],
                                             rhs=NEAR[:, bass.ds(w[t // GT], 1), 0:D].rearrange("p a f -> p (a f)"),
                                             start=False, stop=True, skip_group_check=True)
                        last.then_inc(s["h_ps"][h], 1)
                        pe.wait_ge(s["relu_ready"][h], n)
                        for q in range(GT):
                            last = pe.transpose(b0[:, q * P:(q + 1) * P],
                                                zr[h][:, 2 * q:2 * q + 2, :].rearrange("p t f -> p (t f)"), ident[:])
                        last.then_inc(s["relu_turned"][h], 1)
                        pe.wait_ge(s["relu_t"][h], n)
                        for q in range(GT):
                            last = pe.matmul(b1_[:, q * P:(q + 1) * P], lhsT=zr_t[h][:, q, :], rhs=wm2_diag[:, l, :],
                                             start=True, stop=True)
                        last.then_inc(s["v_ps"][h], 1)
                        pe.wait_ge(s["m_ready"][h], n)
                        for g in range(2):
                            for j in range(GT):
                                t = g * GT + j
                                last = pe.matmul(b2_[:, g * D:(g + 1) * D], lhsT=onehot[h][:, t, :], rhs=z[h][:, t, :],
                                                 start=(j == 0), stop=(j == GT - 1))
                        last.then_inc(s["acc_ps"][h], 1)

                    with pe.Fori(0, NPAIR) as i:
                        for h in range(2):
                            step(h, i)

        def gate_pass():
            s = {n: [sem(f"gate_{n}{h}") for h in range(2)] for n in (
                "rec_in", "far_ready", "e_ready", "onehot_ready", "turned", "turned_sb", "h_ps", "z_ready", "expf",
                "neg", "exps", "plus", "recip", "logs", "soft", "m_ready", "acc_ps", "acc_added")}
            rows = slot_rows[1]
            recb = [r[:].rearrange("p g j f -> p (g j f)")[:, 0:GT * RB].rearrange("p (j f) -> p j f", f=RB) for r in rec]

            with nc.Block() as block:
                @block.sync
                def _(sp):
                    def load(h, i, first):
                        if not first:
                            sp.wait_ge(s["onehot_ready"][h], i)
                            sp.wait_ge(s["e_ready"][h], i)
                            sp.wait_ge(s["z_ready"][h], i)
                        sp.dma_start(recb[h].rearrange("p j f -> p (j f)"),
                                     rows[:, bass.ds(2 * i + h, 1), :].rearrange("p a f -> p (a f)"),
                                     ).then_inc(s["rec_in"][h], 16)

                    for h in range(2):
                        load(h, 0, True)
                    with sp.Fori(1, NPAIR1) as i:
                        for h in range(2):
                            load(h, i, False)

                @block.gpsimd
                def _(pool):
                    def gather(h, i, first):
                        pool.wait_ge(s["rec_in"][h], 16 * (i + 1))
                        if not first:
                            pool.wait_ge(s["z_ready"][h], i)
                        pool.sem_inc(turn, 1)
                        for t in range(GT):
                            pool.indirect_dma_start(
                                out=far_in[h][:, 2 * t:2 * t + 2, :].rearrange("p t f -> p (t f)"), out_offset=None,
                                in_=table2, in_offset=bass.IndirectOffsetOnAxis(
                                    ap=recb[h][:, t, 1:2].bitcast(I32), axis=0)).then_inc(s["far_ready"][h], 16)

                    for h in range(2):
                        gather(h, 0, True)
                    with pool.Fori(1, NPAIR1) as i:
                        for h in range(2):
                            gather(h, i, False)

                @block.vector
                def _(dve):
                    def step(h, i):
                        n = i + 1
                        dve.wait_ge(s["rec_in"][h], 16 * n)
                        w = dve.value_load(window_of[0:1, 1, bass.ds(2 * i + h, 1)], min_val=0, max_val=NW - 1)
                        equal_nodes(dve, onehot[h][:, 0:GT, :], w, recb[h][:, :, 0:1]).then_inc(s["onehot_ready"][h], 1)
                        dve.wait_ge(s["far_ready"][h], 64 * n)
                        dve.wait_ge(s["h_ps"][h], n)
                        dve.tensor_tensor(z[h][:].rearrange("p t f -> p (t f)"), banks[4 * h + 3][:],
                                          far_in[h][:].rearrange("p t f -> p (t f)"),
                                          ALU.add).then_inc(s["z_ready"][h], 1)
                        dve.wait_ge(s["z_ready"][h], n)
                        zf = z[h][:].rearrange("p (t k) f -> p t k f", k=2)
                        dve.scalar_tensor_tensor(out=zz[h][:, 0:GT, :], in0=zf[:, :, 1, :], scalar=-1.0, in1=zf[:, :, 1, :],
                                                 op0=ALU.mult, op1=ALU.min).then_inc(s["neg"][h], 1)
                        dve.wait_ge(s["expf"][h], n)
                        dve.tensor_scalar(zr[h][:, 0:GT, :], zr[h][:, 0:GT, :], 1.0, None, ALU.add).then_inc(s["plus"][h], 1)
                        dve.wait_ge(s["plus"][h], n)
                        dve.reciprocal(zr[h][:, 0:GT, :], zr[h][:, 0:GT, :]).then_inc(s["recip"][h], 1)
                        dve.wait_ge(s["recip"][h], n)
                        dve.wait_ge(s["logs"][h], n)
                        dve.scalar_tensor_tensor(out=zz[h][:, GT:, :], in0=zf[:, :, 1, :], scalar=0.0, in1=zz[h][:, 0:GT, :],
                                                 op0=ALU.max, op1=ALU.add).then_inc(s["soft"][h], 1)
                        dve.wait_ge(s["soft"][h], n)
                        dve.tensor_tensor(zr[h][:, GT:, :], zz[h][:, GT:, :], zr[h][:, 0:GT, :],
                                          ALU.mult).then_inc(s["m_ready"][h], 1)
                        dve.wait_ge(s["acc_ps"][h], n)
                        row = ACC[:, bass.ds(w, 1), :].rearrange("p a f -> p (a f)")
                        dve.tensor_tensor(row, row, banks[4 * h + 1][:, 0:D], ALU.add).then_inc(s["acc_added"][h], 1)
                        dve.wait_ge(s["acc_added"][h], n)

                    with dve.Fori(0, NPAIR1) as i:
                        for h in range(2):
                            step(h, i)

                @block.scalar
                def _(act):
                    def step(h, i):
                        n = i + 1
                        act.wait_ge(s["rec_in"][h], 16 * n)
                        act.activation(e_flat[h][:].rearrange("p (j f) -> p j f", j=GT), recb[h][:, :, 2:2 + E32],
                                       ACT.Copy).then_inc(s["e_ready"][h], 1)
                        act.wait_ge(s["turned"][h], n)
                        act.activation(onehot_t[h][:, 0:GT, :].rearrange("p t f -> p (t f)"), banks[4 * h][:], ACT.Copy)
                        act.activation(e_t[h][:], banks[4 * h + 2][:, 0:P], ACT.Copy).then_inc(s["turned_sb"][h], 1)
                        act.wait_ge(s["z_ready"][h], n)
                        zf = z[h][:].rearrange("p (t k) f -> p t k f", k=2)
                        act.activation(zr[h][:, 0:GT, :], zf[:, :, 0, :], ACT.Exp, scale=-1.0).then_inc(s["expf"][h], 1)
                        act.wait_ge(s["neg"][h], n)
                        act.activation(zz[h][:, 0:GT, :], zz[h][:, 0:GT, :], ACT.Exp).then_inc(s["exps"][h], 1)
                        act.wait_ge(s["exps"][h], n)
                        act.activation(zz[h][:, 0:GT, :], zz[h][:, 0:GT, :], ACT.Ln, bias=1.0).then_inc(s["logs"][h], 1)

                    with act.Fori(0, NPAIR1) as i:
                        for h in range(2):
                            step(h, i)

                @block.tensor
                def _(pe):
                    def step(h, i):
                        n = i + 1
                        b0, b1_, b2_, b3 = banks[4 * h:4 * h + 4]
                        w = pe.value_load(window_of[0:1, 1, bass.ds(2 * i + h, 1)], min_val=0, max_val=NW - 1)
                        pe.wait_ge(s["e_ready"][h], n)
                        pe.transpose(b2_[:, 0:P], e_flat[h][:], ident[:])
                        pe.wait_ge(s["onehot_ready"][h], n)
                        for t in range(GT):
                            last = pe.transpose(b0[:, t * P:(t + 1) * P], onehot[h][:, t, :], ident[:])
                        last.then_inc(s["turned"][h], 1)
                        pe.wait_ge(s["turned_sb"][h], n)
                        pe.matmul(b3[:], lhsT=e_t[h][:], rhs=wge_diag[:], start=True, stop=False, skip_group_check=True)
                        for t in range(GT):
                            last = pe.matmul(b3[:, t * 2 * D:(t + 1) * 2 * D], lhsT=onehot_t[h][:, t, :],
                                             rhs=NEAR[:, bass.ds(w, 1), :].rearrange("p a f -> p (a f)"),
                                             start=False, stop=True, skip_group_check=True)
                        last.then_inc(s["h_ps"][h], 1)
                        pe.wait_ge(s["m_ready"][h], n)
                        for t in range(GT):
                            last = pe.matmul(b1_[:, 0:D], lhsT=onehot[h][:, t, :], rhs=zr[h][:, GT + t, :],
                                             start=(t == 0), stop=(t == GT - 1))
                        last.then_inc(s["acc_ps"][h], 1)

                    with pe.Fori(0, NPAIR1) as i:
                        for h in range(2):
                            step(h, i)

        def sum_pass(name, with_edges):
            s = {n: [sem(f"{name}_{n}{h}") for h in range(2)] for n in (
                "rec_in", "far_ready", "onehot_ready", "acc_ps", "acc_mid", "acc_mid2", "acc_mid3", "acc_added")}
            rows = slot_rows[0]
            EW = E32 + 1

            with nc.Block() as block:
                @block.sync
                def _(sp):
                    def load(h, i, first):
                        if not first:
                            sp.wait_ge(s["acc_ps"][h], i)
                        sp.dma_start(rec[h][:].rearrange("p g j f -> p g (j f)"),
                                     rows[:, bass.ds(4 * i + 2 * h, 2), :]).then_inc(s["rec_in"][h], 16)

                    for h in range(2):
                        load(h, 0, True)
                    with sp.Fori(1, NPAIR) as i:
                        for h in range(2):
                            load(h, i, False)

                @block.gpsimd
                def _(pool):
                    def gather(h, i, first):
                        pool.wait_ge(s["rec_in"][h], 16 * (i + 1))
                        if not first:
                            pool.wait_ge(s["acc_ps"][h], i)
                        pool.sem_inc(turn, 1)
                        for t in range(2 * GT):
                            pool.indirect_dma_start(
                                out=far_in[h][:, t, :], out_offset=None, in_=table,
                                in_offset=bass.IndirectOffsetOnAxis(
                                    ap=rec[h][:, t // GT, t % GT, 1:2].bitcast(I32), axis=0),
                            ).then_inc(s["far_ready"][h], 16)

                    for h in range(2):
                        gather(h, 0, True)
                    with pool.Fori(1, NPAIR) as i:
                        for h in range(2):
                            gather(h, i, False)

                @block.vector
                def _(dve):
                    def step(h, i):
                        n = i + 1
                        dve.wait_ge(s["rec_in"][h], 16 * n)
                        w = [dve.value_load(window_of[0:1, 0, bass.ds(4 * i + 2 * h + g, 1)], min_val=0, max_val=NW - 1)
                             for g in range(2)]
                        for g in range(2):
                            last = equal_nodes(dve, onehot[h][:, g * GT:(g + 1) * GT, :], w[g], rec[h][:, g, :, 0:1])
                        last.then_inc(s["onehot_ready"][h], 1)
                        dve.wait_ge(s["acc_ps"][h], n)
                        for g in range(2):
                            row = ACC[:, bass.ds(w[g], 1), :].rearrange("p a f -> p (a f)")
                            mark = s["acc_added" if g else "acc_mid"][h]
                            dve.tensor_tensor(row, row, banks[2 * h][:, g * D:(g + 1) * D], ALU.add).then_inc(mark, 1)
                            dve.wait_ge(mark, n)
                            if with_edges:
                                row = ACC2[:, bass.ds(w[g], 1), :].rearrange("p a f -> p (a f)")
                                mark = s["acc_mid3" if g else "acc_mid2"][h]
                                dve.tensor_tensor(row, row, banks[2 * h + 1][:, g * EW:(g + 1) * EW],
                                                  ALU.add).then_inc(mark, 1)
                                dve.wait_ge(mark, n)

                    with dve.Fori(0, NPAIR) as i:
                        for h in range(2):
                            step(h, i)

                @block.tensor
                def _(pe):
                    def step(h, i):
                        n = i + 1
                        pe.wait_ge(s["onehot_ready"][h], n)
                        pe.wait_ge(s["rec_in"][h], 16 * n)
                        for g in range(2 if with_edges else 0):
                            for j in range(GT):
                                pe.matmul(banks[2 * h + 1][:, g * EW:(g + 1) * EW], lhsT=onehot[h][:, g * GT + j, :],
                                          rhs=rec[h][:, g, j, A32:A32 + EW], start=(j == 0), stop=(j == GT - 1))
                        pe.wait_ge(s["far_ready"][h], 128 * n)
                        for g in range(2):
                            for j in range(GT):
                                last = pe.matmul(banks[2 * h][:, g * D:(g + 1) * D], lhsT=onehot[h][:, g * GT + j, :],
                                                 rhs=far_in[h][:, g * GT + j, :], start=(j == 0), stop=(j == GT - 1))
                        last.then_inc(s["acc_ps"][h], 1)

                    with pe.Fori(0, NPAIR) as i:
                        for h in range(2):
                            step(h, i)

        node_block(lambda dve: norm_relu(dve, H[:], X[:]))
        for l in range(LAYERS):
            with new_stage():
                linear(f"tables{l}", wtab[:, l, :], 2 * D, D, NEAR, D, table)

            def before_edges(dve, l=l):
                then(dve, dve.tensor_tensor(S, S, over(biases[:, l, :]), ALU.add))
                then(dve, dve.memset(ACC[:], 0.0))
            node_block(before_edges)
            with new_stage():
                mpnn_pass(l)
            with new_stage():
                linear(f"update{l}", wupd[:, l, :], D, P, NEAR[:, :, D:], D)

            def update(dve, l=l):
                T = NEAR[:, :, D:]
                then(dve, dve.tensor_tensor(T, T, over(biases[:, 2 * LAYERS + l, :]), ALU.add))
                norm_relu(dve, ACC[:], T)
                then(dve, dve.tensor_tensor(H[:], H[:], ACC[:], ALU.add))
                if l == LAYERS - 1:
                    then(dve, dve.tensor_tensor(X[:], X[:], H[:], ALU.add))
                    norm_relu(dve, H[:], X[:])
            node_block(update)

        with new_stage():
            linear("gate_tables", wgate[:], 4 * D, D, NEAR, 2 * D, table2)

        def before_gate(dve):
            then(dve, dve.tensor_tensor(
                NEAR[:], NEAR[:], gate_bias[:].rearrange("p k f -> p (k f)").rearrange("p (a f) -> p a f", a=1)
                .broadcast_to([P, NW, 2 * D]), ALU.add))
            then(dve, dve.memset(ACC[:], 0.0))
        node_block(before_gate)
        with new_stage():
            gate_pass()

        bn_asked, bn_done = sem("bn_asked"), sem("bn_done")
        table_ready, table_out = sem("table_ready"), sem("table_out")
        bn = sb("bn", [P, 3, D])

        def send_state(sp, n):
            sp.wait_ge(table_ready, n)
            sp.dma_start(table.rearrange("(w p) f -> p w f", p=P), H[:]).then_inc(table_out, 16)
            sp.wait_ge(table_out, 16 * n)

        with nc.Block() as block:
            @block.tensor
            def _(pe):
                for n in range(2):
                    pe.wait_ge(bn_asked, n + 1)
                    pe.matmul(banks[n][:, 0:D], lhsT=ones[:], rhs=bn[:, n, :], start=True, stop=True).then_inc(bn_done, 1)

            @block.vector
            def _(dve):
                dve.tensor_reduce(bn[:, 0, :], ACC[:].rearrange("p w f -> p f w"), AX, ALU.add).then_inc(bn_asked, 1)
                dve.wait_ge(bn_done, 1)
                then(dve, dve.tensor_scalar(bn[:, 2, :], banks[0][:, 0:D], 1.0 / N, None, ALU.mult))
                then(dve, dve.tensor_tensor(ACC[:], ACC[:], over(bn[:, 2, :]), ALU.subtract))
                then(dve, dve.tensor_scalar(ACC[:, NW - 1, :], ACC[:, NW - 1, :], valid[:, 0:1], None, ALU.mult))
                then(dve, dve.tensor_tensor(S, ACC[:], ACC[:], ALU.mult))
                dve.tensor_reduce(bn[:, 1, :], S.rearrange("p w f -> p f w"), AX, ALU.add).then_inc(bn_asked, 1)
                dve.wait_ge(bn_done, 2)
                then(dve, dve.tensor_scalar(bn[:, 2, :], banks[1][:, 0:D], 1.0 / N, EPS, ALU.mult, ALU.add))
                root(dve, bn[:, 2, :])
                then(dve, dve.reciprocal(bn[:, 2, :], bn[:, 2, :]))
                then(dve, dve.tensor_tensor(bn[:, 2, :], bn[:, 2, :], gb[:, 0, :], ALU.mult))
                then(dve, dve.tensor_tensor(ACC[:], ACC[:], over(bn[:, 2, :]), ALU.mult))
                then(dve, dve.tensor_tensor(ACC[:], ACC[:], over(gb[:, 1, :]), ALU.add))
                then(dve, dve.tensor_tensor(ACC[:], ACC[:], H[:], ALU.add))
                then(dve, dve.tensor_tensor(X[:], X[:], ACC[:], ALU.add))
                norm_relu(dve, H[:], X[:])
                dve.memset(ACC[:], 0.0).then_inc(table_ready, 1)

            @block.scalar
            def _(act):
                take_roots(act)

            @block.sync
            def _(sp):
                send_state(sp, 1)

        with new_stage():
            sum_pass("sum", False)

        with nc.Block() as block:
            @block.vector
            def _(dve):
                then(dve, dve.tensor_tensor(X[:], X[:], ACC[:], ALU.add))
                norm_relu(dve, H[:], X[:])
                then(dve, dve.memset(ACC2[:], 0.0))
                dve.memset(ACC[:], 0.0).then_inc(table_ready, 1)

            @block.scalar
            def _(act):
                take_roots(act)

            @block.sync
            def _(sp):
                send_state(sp, 2)

        with new_stage():
            sum_pass("last", True)

        staged, turned, turned_in = sem("out_staged"), sem("out_turned"), sem("out_turned_in")
        turned2, turned2_in = sem("out_turned2"), sem("out_turned2_in")
        hidden, hidden_in, product, summed = sem("out_hidden"), sem("out_hidden_in"), sem("out_product"), sem("out_summed")
        out_done = sem("out_done")
        stage2 = sb("stage2", [P, WC, E32 + 1])
        stage2_t = sb("stage2_t", [E32 + 1, WC, P])
        acc_t = sb("acc_t", [D, WC, P])
        hidden_t = sb("hidden_t", [P, WC, P])
        HALVES = [(0, 4), (4, WC)]
        EW = E32 + 1

        with nc.Block() as block:
            @block.vector
            def _(dve):
                def put(i, n, first):
                    if not first:
                        dve.wait_ge(turned, i)
                        dve.wait_ge(turned2, i)
                    dve.tensor_copy(stage[:, :, 0:D], H[:, bass.ds(i * WC, WC), :]).then_inc(staged, 1)
                    dve.tensor_copy(stage[:, :, D:], ACC[:, bass.ds(i * WC, WC), :]).then_inc(staged, 1)
                    dve.tensor_copy(stage2[:], ACC2[:, bass.ds(i * WC, WC), :]).then_inc(staged, 1)
                    dve.wait_ge(product, n)
                    dve.tensor_tensor(S[:, bass.ds(i * WC, WC), :], X[:, bass.ds(i * WC, WC), :],
                                      banks[6][:, 0:WC * D].rearrange("p (j f) -> p j f", f=D),
                                      ALU.add).then_inc(summed, 1)

                put(0, 1, True)
                with dve.Fori(1, NWC) as i:
                    put(i, i + 1, False)
                dve.wait_ge(summed, NWC)
                dve.tensor_tensor(S, S, over(c2r[:]), ALU.add).then_inc(out_done, 1)

            @block.tensor
            def _(pe):
                def go(n):
                    pe.wait_ge(staged, 3 * n)
                    for j in range(WC):
                        last = pe.transpose(banks[j // 4][:, (j % 4) * P:(j % 4 + 1) * P], stage[:, j, :], ident[:])
                    last.then_inc(turned, 1)
                    for j in range(WC):
                        last = pe.transpose(banks[2 + j // 4][0:EW, (j % 4) * P:(j % 4 + 1) * P], stage2[:, j, :], ident[:])
                    last.then_inc(turned2, 1)
                    pe.wait_ge(turned_in, 6 * n)
                    for q, (a, b) in enumerate(HALVES):
                        pe.matmul(banks[4 + q][:, 0:(b - a) * P], lhsT=v1a[:],
                                  rhs=acc_t[:, a:b, :].rearrange("p j f -> p (j f)"), start=True, stop=False)
                        last = pe.matmul(banks[4 + q][:, 0:(b - a) * P], lhsT=v1b[:],
                                         rhs=stage2_t[:, a:b, :].rearrange("p j f -> p (j f)"), start=False, stop=True)
                    last.then_inc(hidden, 1)
                    pe.wait_ge(hidden_in, 2 * n)
                    for j in range(WC):
                        pe.matmul(banks[6][:, j * D:(j + 1) * D], lhsT=stage_t[0:D, j, :], rhs=v2a[:], start=True, stop=False)
                        last = pe.matmul(banks[6][:, j * D:(j + 1) * D], lhsT=hidden_t[:, j, :], rhs=v2b[:],
                                         start=False, stop=True)
                    last.then_inc(product, 1)

                go(1)
                with pe.Fori(1, NWC) as i:
                    pe.wait_ge(summed, i)
                    go(i + 1)

            @block.scalar
            def _(act):
                with act.Fori(0, NWC) as i:
                    n = i + 1
                    act.wait_ge(turned, n)
                    act.wait_ge(turned2, n)
                    for q, (a, b) in enumerate(HALVES):
                        act.activation(stage_t[0:D, a:b, :].rearrange("p j f -> p (j f)"),
                                       banks[q][0:D, 0:(b - a) * P], ACT.Copy).then_inc(turned_in, 1)
                        act.activation(acc_t[:, a:b, :].rearrange("p j f -> p (j f)"),
                                       banks[q][D:P, 0:(b - a) * P], ACT.Copy).then_inc(turned_in, 1)
                        act.activation(stage2_t[:, a:b, :].rearrange("p j f -> p (j f)"),
                                       banks[2 + q][0:EW, 0:(b - a) * P], ACT.Copy).then_inc(turned_in, 1)
                    act.wait_ge(hidden, n)
                    for q, (a, b) in enumerate(HALVES):
                        act.activation(hidden_t[:, a:b, :].rearrange("p j f -> p (j f)"),
                                       banks[4 + q][:, 0:(b - a) * P], ACT.Copy).then_inc(hidden_in, 1)

            @block.sync
            def _(sp):
                sp.wait_ge(out_done, 1)
                sp.dma_start(out[0:(NW - 1) * P, :].rearrange("(w p) f -> p w f", p=P), S[:, 0:NW - 1, :]).then_inc(table_out, 16)
                sp.dma_start(out[(NW - 1) * P:, :], S[0:LASTW, NW - 1, :]).then_inc(table_out, 16)
                sp.wait_ge(table_out, 64)


_INS = ['x', 'src', 'dst', 'edge_attr_16', 'edge_attr_32', 'L0_gnn_msg_w1', 'L0_gnn_msg_b1', 'L0_gnn_msg_w2',
        'L0_gnn_msg_b2', 'L0_gnn_upd_w', 'L0_gnn_upd_b', 'L1_gnn_W_f', 'L1_gnn_b_f', 'L1_gnn_W_s', 'L1_gnn_b_s',
        'L1_gnn_gamma', 'L1_gnn_beta', 'L3_gnn_W1', 'L3_gnn_b1', 'L3_gnn_W2', 'L3_gnn_b2']


def kernel(**inputs):
    import numpy as _np
    import concourse.bacc as _bacc
    from concourse import mybir as _mybir
    from concourse.bass_utils import run_bass_kernel_spmd as _run

    nc = _bacc.Bacc("TRN2", target_bir_lowering=False, num_devices=1)
    arrays, args = {}, []
    for name in _INS:
        a = _np.ascontiguousarray(inputs[name])
        arrays[f"in_{name}"] = a
        args.append(nc.dram_tensor(f"in_{name}", a.shape, _mybir.dt.from_np(a.dtype), kind="ExternalInput").ap())
    args.append(nc.dram_tensor("out_x", (N, D), F32, kind="ExternalOutput").ap())
    build(nc, *args)
    r = _run(nc, [arrays], core_ids=[0])
    return r.results[0]["out_x"]
```

```python
from contextlib import ExitStack, contextmanager

import concourse.bass as bass
from concourse import mybir

F32 = mybir.dt.float32
I32 = mybir.dt.int32
BF16 = mybir.dt.bfloat16
ALU = mybir.AluOpType
ACT = mybir.ActivationFunctionType
AX = mybir.AxisListType.X

P = 128
N = 6250
E = 200000
D = 64
E16, E32 = 16, 32
HID = 128
LAYERS = 3
EPS = 1e-5
NW = -(-N // P)
NPAD = NW * P
LASTW = N - (NW - 1) * P
GT = 4
GE = GT * P
NG = -(-E // GE) + NW
NG += -NG % 4
NS = NG * GE
CF = E // P
TAIL = E - P * CF
C = CF + (TAIL > 0)
CH = 11
assert CF % (2 * CH) == 0 and TAIL > 0
NCH = CF // CH // 2
RA = 52
RB = 34
A16, A32 = 2, 2 + E16
WC = 7
NWC = NW // WC
assert NW % WC == 0 and NG <= 4 * P
FILL = 110
assert (NS // P) % FILL == 0


def build(nc, x, src, dst, ea16, ea32, w1, b1, w2, b2, wu, bu, wf, bf, ws, bs, gamma, beta, v1, c1, v2, c2, out):
    ctx = ExitStack()

    def sb(name, shape, dt=F32):
        return ctx.enter_context(nc.sbuf_tensor(name, shape, dt))

    stage_sems = [[]]

    def sem(name):
        stage_sems[-1].append(nc.alloc_semaphore(name))
        return stage_sems[-1][-1]

    @contextmanager
    def new_stage():
        stage_sems.append([])
        yield
        nc.clear_and_free_semaphores(stage_sems.pop())
        nc.all_engine_barrier()

    def dram(name, shape, dt=F32):
        return nc.dram_tensor(name, shape, dt, kind="Internal").ap()

    with ctx:
        by_dst = dram("by_dst", [NS, RA])
        by_src = dram("by_src", [NS, RB])
        table = dram("table", [NPAD, D])
        table2 = dram("table2", [NPAD, 2 * D])
        base_row = [dram(f"base_row{k}", [1, 4 * P]) for k in range(2)]
        window_row = [dram(f"window_row{k}", [1, 4 * P], I32) for k in range(2)]

        X = sb("X", [P, NW, D])
        iota_f = sb("iota_f", [P, P])
        iota_b = sb("iota_b", [P, P], BF16)
        ident = sb("ident", [P, P])
        ident_b = sb("ident_b", [P, P], BF16)
        upper = sb("upper", [P, P])
        ones = sb("ones", [P, P])
        bins = sb("bins", [P, NW])
        valid = sb("valid", [P, 1])
        group_ids = sb("group_ids", [P, 4])
        window_of = sb("window_of", [1, 2, 4 * P], I32)
        window_base = sb("window_base", [P, 2, 4 * P])

        wtab = sb("wtab", [D, LAYERS, 2 * D])
        wupd = sb("wupd", [2 * D, LAYERS, D])
        we = sb("we", [E16, LAYERS, D])
        wm2 = sb("wm2", [D, LAYERS, D])
        we_diag = sb("we_diag", [P, LAYERS, 8 * D])
        wm2_diag = sb("wm2_diag", [P, LAYERS, 2 * D])
        biases = sb("biases", [P, 3 * LAYERS, D])
        gate_bias = sb("gate_bias", [P, 2, D])
        gb = sb("gb", [P, 2, D])
        wgate = sb("wgate", [D, 4 * D])
        wge_diag = sb("wge_diag", [P, 4 * 2 * D])
        v1a = sb("v1a", [D, HID])
        v1b = sb("v1b", [E32 + 1, HID])
        v2a = sb("v2a", [D, D])
        v2b = sb("v2b", [HID, D])
        c2r = sb("c2r", [P, D])
        wmean = sb("wmean", [P, 5 * LAYERS + 1])
        bmean = sb("bmean", [P, 3 * LAYERS])

        stage = sb("stage", [P, WC, P])
        stage_t = sb("stage_t", [P, WC, P])
        small = sb("small", [P, 4, NW])
        small_i = sb("small_i", [P, NW], I32)

        banks = [ctx.enter_context(nc.psum_tensor(f"bank{i}", [P, 512], F32)) for i in range(7)]
        bank_bf = ctx.enter_context(nc.psum_tensor("bank_bf", [P, 1024], BF16))

        turn = sem("turn")

        vector_step = sem("vector_step")
        vector_count = [0]

        def then(dve, ins):
            vector_count[0] += 1
            ins.then_inc(vector_step, 1)
            dve.wait_ge(vector_step, vector_count[0])

        order = ExitStack()
        keys_i = [order.enter_context(nc.sbuf_tensor(f"keys_i{k}", [P, C], I32)) for k in range(2)]
        key_f = order.enter_context(nc.sbuf_tensor("key_f", [P, C], F32))
        win_f = order.enter_context(nc.sbuf_tensor("win_f", [P, C], F32))
        mask = order.enter_context(nc.sbuf_tensor("mask", [P, C], I32))
        run = order.enter_context(nc.sbuf_tensor("run", [P, C], F32))
        place_f = order.enter_context(nc.sbuf_tensor("place_f", [P, C], F32))
        place = [order.enter_context(nc.sbuf_tensor(f"place{k}", [P, C], I32)) for k in range(2)]
        hist = order.enter_context(nc.sbuf_tensor("hist", [P, NW], F32))
        ends = order.enter_context(nc.sbuf_tensor("ends", [P, NW], F32))
        before = order.enter_context(nc.sbuf_tensor("before", [P, 4, NW], F32))
        win4 = order.enter_context(nc.sbuf_tensor("win4", [P, 4], F32))
        base4 = order.enter_context(nc.sbuf_tensor("base4", [P, 4], F32))
        win4_i = order.enter_context(nc.sbuf_tensor("win4_i", [P, 4], I32))
        st16 = [order.enter_context(nc.sbuf_tensor(f"st16_{k}", [P, CH, E16], F32)) for k in range(2)]
        st32 = [order.enter_context(nc.sbuf_tensor(f"st32_{k}", [P, CH, E32], F32)) for k in range(2)]
        recs = [order.enter_context(nc.sbuf_tensor(f"recs{k}", [P, CH, RA], F32)) for k in range(2)]
        slots = [order.enter_context(nc.sbuf_tensor(f"slots{k}", [P, CH], I32)) for k in range(2)]

        keys_in = sem("keys_in")
        keys_loaded = sem("keys_loaded")
        windows_out = [sem(f"windows_out{k}") for k in range(2)]
        hist_ready = [sem(f"hist_ready{k}") for k in range(2)]
        hist_ps = [sem(f"hist_ps{k}") for k in range(2)]
        win4_ready = [sem(f"win4_ready{k}") for k in range(2)]
        mask_ready = [sem(f"mask_ready{k}") for k in range(2)]
        run_ready = [sem(f"run_ready{k}") for k in range(2)]
        picked = [sem(f"picked{k}") for k in range(2)]
        counts_ps, prefix_ps = banks[0][:, 0:NW], banks[1][:, 0:NW]

        def rank_vector(dve, k):
            then(dve, dve.tensor_copy(win_f[:], keys_i[k][:]))
            then(dve, dve.tensor_scalar(mask[:], keys_i[k][:], 7, None, ALU.arith_shift_right))
            then(dve, dve.tensor_copy(win_f[:], mask[:]))
            then(dve, dve.memset(place_f[:], 1.0))
            with dve.Fori(0, NW) as b:
                dve.tensor_scalar(run[:], win_f[:], bins[:, bass.ds(b, 1)], None, ALU.is_equal, ALU.add,
                                  accum_out=hist[:, bass.ds(b, 1)]).then_inc(hist_ready[k], 1)
                dve.wait_ge(hist_ready[k], b + 1)
            dve.wait_ge(hist_ps[k], 1)
            groups, start, low, cum = small[:, 0, :], small[:, 1, :], small[:, 2, :], small[:, 3, :]
            then(dve, dve.tensor_scalar(low, counts_ps, float(GE - 1), None, ALU.add))
            then(dve, dve.tensor_copy(small_i[:], low))
            then(dve, dve.tensor_scalar(small_i[:], small_i[:], 9, None, ALU.arith_shift_right))
            then(dve, dve.tensor_copy(groups, small_i[:]))
            then(dve, dve.tensor_tensor_scan(ends[:], groups, groups, 0.0, ALU.add, ALU.max))
            then(dve, dve.tensor_tensor(start, ends[:], groups, ALU.subtract))
            then(dve, dve.scalar_tensor_tensor(out=cum, in0=start, scalar=float(GE), in1=prefix_ps,
                                               op0=ALU.mult, op1=ALU.add))
            then(dve, dve.tensor_tensor(before[:], ends[:].rearrange("p (a w) -> p a w", a=1).broadcast_to([P, 4, NW]),
                                        group_ids[:].rearrange("p (g a) -> p g a", a=1).broadcast_to([P, 4, NW]),
                                        ALU.is_le))
            then(dve, dve.tensor_reduce(win4[:], before[:], AX, ALU.add))
            then(dve, dve.tensor_scalar(win4[:], win4[:], float(NW - 1), None, ALU.min))
            dve.tensor_scalar(base4[:], win4[:], float(P), None, ALU.mult).then_inc(win4_ready[k], 1)
            dve.tensor_copy(win4_i[:], win4[:]).then_inc(win4_ready[k], 1)
            with dve.Fori(0, NW) as b:
                n = b + 1
                dve.tensor_scalar(mask[:], win_f[:], bins[:, bass.ds(b, 1)], None,
                                  ALU.is_equal).then_inc(mask_ready[k], 1)
                dve.wait_ge(mask_ready[k], n)
                dve.tensor_tensor_scan(run[:], mask[:], mask[:], cum_of(b), ALU.add, ALU.max).then_inc(run_ready[k], 1)
                dve.wait_ge(run_ready[k], n)
                dve.sem_inc(turn, 1)
                dve.copy_predicated(place_f[:], mask[:], run[:]).then_inc(picked[k], 1)
                dve.wait_ge(picked[k], n)
            then(dve, dve.tensor_scalar(place[k][:], place_f[:], -1.0, None, ALU.add))

        def cum_of(b):
            return small[:, 3, bass.ds(b, 1)]

        def rank_tensor(pe, k):
            pe.wait_ge(hist_ready[k], NW)
            pe.matmul(counts_ps, lhsT=ones[:], rhs=hist[:], start=True, stop=True)
            pe.matmul(prefix_ps, lhsT=upper[:], rhs=hist[:], start=True, stop=True).then_inc(hist_ps[k], 1)

        def rank_windows(sp, k):
            sp.wait_ge(win4_ready[k], 2)
            sp.dma_start(window_row[k].rearrange("a (p c) -> (a p) c", p=P), win4_i[:]).then_inc(windows_out[k], 16)
            sp.dma_start(base_row[k].rearrange("a (p c) -> (a p) c", p=P), base4[:]).then_inc(windows_out[k], 16)
            sp.wait_ge(windows_out[k], 32)
            sp.dma_start(window_of[:, k, :], window_row[k]).then_inc(windows_out[k], 16)
            sp.dma_start(window_base[:, k, :], base_row[k].broadcast_to([P, 4 * P])).then_inc(windows_out[k], 16)
            sp.wait_ge(windows_out[k], 64)

        weights_in = sem("weights_in")
        blocks_in = sem("blocks_in")
        iota_ready = sem("iota_ready")
        consts_ready = sem("consts_ready")
        zeroed = sem("zeroed")
        centred = sem("centred")
        pool_step = sem("pool_step")
        fill_ready = sem("fill_ready")
        filled = sem("filled")
        n_weights = [0]

        with ExitStack() as stack:
            ids_i = stack.enter_context(nc.sbuf_tensor("ids_i", [P, P], I32))
            fills = [stack.enter_context(nc.sbuf_tensor(f"fill{k}", [P, FILL, width], F32))
                     for k, width in enumerate((RA, RB))]
            block = stack.enter_context(nc.Block())

            @block.gpsimd
            def _(pool):
                pool.iota(ids_i[:], pattern=[[1, P]], base=0, channel_multiplier=0).then_inc(iota_ready, 1)
                pool.iota(group_ids[:].bitcast(I32), pattern=[[1, 4]], base=0, channel_multiplier=4).then_inc(iota_ready, 1)
                pool.memset(ones[:], 1.0).then_inc(pool_step, 1)
                pool.memset(upper[:], 1.0).then_inc(pool_step, 1)
                pool.memset(ident[:], 0.0).then_inc(pool_step, 1)
                pool.memset(valid[:], 1.0).then_inc(pool_step, 1)
                pool.memset(fills[0][:], 0.0).then_inc(pool_step, 1)
                pool.memset(fills[1][:], 0.0).then_inc(pool_step, 1)
                pool.wait_ge(pool_step, 6)
                pool.memset(fills[0][:, :, 0:1], -1.0).then_inc(fill_ready, 1)
                pool.memset(fills[1][:, :, 0:1], -1.0).then_inc(fill_ready, 1)
                pool.affine_select(out=ident[:], in_=ident[:], compare_op=ALU.not_equal, fill=1.0, base=0,
                                   pattern=[[-1, P]], channel_multiplier=1).then_inc(consts_ready, 1)
                pool.affine_select(out=upper[:], in_=upper[:], compare_op=ALU.is_ge, fill=0.0, base=-1,
                                   pattern=[[1, P]], channel_multiplier=-1).then_inc(consts_ready, 1)
                pool.affine_select(out=valid[:], in_=valid[:], compare_op=ALU.is_ge, fill=0.0, base=LASTW - 1,
                                   pattern=[[0, 1]], channel_multiplier=-1).then_inc(consts_ready, 1)
                pool.memset(X[:], 0.0).then_inc(zeroed, 1)
                pool.memset(wge_diag[:], 0.0).then_inc(zeroed, 1)
                pool.memset(we_diag[:], 0.0).then_inc(zeroed, 1)
                pool.memset(wm2_diag[:], 0.0).then_inc(zeroed, 1)
                pool.memset(stage[:], 0.0).then_inc(zeroed, 1)
                pool.wait_ge(consts_ready, 3)
                pool.wait_ge(zeroed, 5)

            @block.sync
            def _(sp):
                def load(to, frm):
                    n_weights[0] += 16
                    sp.dma_start(to, frm).then_inc(weights_in, 16)

                def load_late(to, frm):
                    sp.dma_start(to, frm).then_inc(blocks_in, 16)

                def spread(v):
                    return v.rearrange("(a n) -> a n", a=1).broadcast_to([P, v.shape[0]])

                sp.wait_ge(keys_in, 1)
                for keys, to in ((dst, keys_i[0]), (src, keys_i[1])):
                    sp.dma_start(to[:, 0:CF], keys[0:P * CF].rearrange("(p c) -> p c", p=P)).then_inc(keys_loaded, 16)
                    sp.dma_start(to[0:TAIL, CF:C], keys[P * CF:].rearrange("(p c) -> p c", c=1)).then_inc(keys_loaded, 16)
                for l in range(LAYERS):
                    load(wtab[:, l, 0:D], w1[l, 0:D, :])
                    load(wtab[:, l, D:], w1[l, D:2 * D, :])
                    load(we[:, l, :], w1[l, 2 * D:, :])
                    load(wm2[:, l, :], w2[l])
                    load(wupd[:, l, :], wu[l])
                    load(biases[:, l, :], spread(b1[l]))
                    load(biases[:, LAYERS + l, :], spread(b2[l]))
                    load(biases[:, 2 * LAYERS + l, :], spread(bu[l]))
                for k, (w, b) in enumerate(((wf, bf), (ws, bs))):
                    load(wgate[:, k * D:(k + 1) * D], w[0:D, :])
                    load(wgate[:, (2 + k) * D:(3 + k) * D], w[D:2 * D, :])
                    load(gate_bias[:, k, :], spread(b))
                load(gb[:, 0, :], spread(gamma))
                load(gb[:, 1, :], spread(beta))
                load(v1a[:], v1[0:D, :])
                load(v1b[0:E32, :], v1[D:, :])
                load(v1b[E32:E32 + 1, :], c1.rearrange("(a n) -> a n", a=1))
                load(v2a[:], v2[0:D, :])
                load(v2b[:], v2[D:, :])
                load(c2r[:], spread(c2))
                sp.wait_ge(zeroed, 5)
                load_late(X[:, 0:NW - 1, :], x[0:(NW - 1) * P, :].rearrange("(w p) f -> p w f", p=P))
                load_late(X[0:LASTW, NW - 1, :], x[(NW - 1) * P:, :])
                for t in range(4):
                    for k, w in enumerate((wf, ws)):
                        load_late(wge_diag[E32 * t:E32 * (t + 1), (2 * t + k) * D:(2 * t + k + 1) * D], w[2 * D:, :])
                sp.wait_ge(weights_in, n_weights[0])
                sp.wait_ge(blocks_in, 16 * 10)
                sp.wait_ge(keys_loaded, 64)
                rank_windows(sp, 0)

            @block.scalar
            def _(act):
                rows = NS // P
                for order_, target in enumerate((by_dst, by_src)):
                    act.wait_ge(fill_ready, order_ + 1)
                    for k in range(rows // FILL):
                        act.dma_start(target.rearrange("(p r) f -> p r f", p=P)[:, k * FILL:(k + 1) * FILL, :],
                                      fills[order_][:]).then_inc(filled, 16)
                act.wait_ge(filled, 32 * (rows // FILL))

            @block.vector
            def _(dve):
                then(dve, dve.memset(keys_i[0][:, CF:C], NPAD))
                dve.memset(keys_i[1][:, CF:C], NPAD).then_inc(keys_in, 1)
                dve.wait_ge(iota_ready, 2)
                dve.tensor_copy(iota_f[:], ids_i[:])
                dve.tensor_copy(iota_b[:], ids_i[:])
                dve.tensor_copy(bins[:], ids_i[:, 0:NW])
                then(dve, dve.tensor_copy(small[:, 0, 0:4], group_ids[:].bitcast(I32)))
                then(dve, dve.tensor_copy(group_ids[:], small[:, 0, 0:4]))
                dve.wait_ge(keys_loaded, 64)
                rank_vector(dve, 0)
                dve.wait_ge(consts_ready, 3)
                then(dve, dve.tensor_copy(ident_b[:], ident[:]))

            @block.tensor
            def _(pe):
                pe.wait_ge(consts_ready, 3)
                rank_tensor(pe, 0)

        def centre_weights(dve):
            dve.wait_ge(weights_in, n_weights[0])
            mats = []
            for l in range(LAYERS):
                mats += [wtab[:, l, 0:D], wtab[:, l, D:], we[:, l, :], wm2[:, l, :], wupd[:, l, :]]
            for k, m in enumerate(mats):
                last = dve.tensor_reduce(wmean[0:m.shape[0], k:k + 1], m, AX, ALU.add)
            then(dve, dve.tensor_reduce(bmean[:], biases[:], AX, ALU.add))
            for k, m in enumerate(mats):
                r = m.shape[0]
                then(dve, dve.tensor_scalar(wmean[0:r, k:k + 1], wmean[0:r, k:k + 1], 1.0 / D, None, ALU.mult))
                last = dve.tensor_scalar(m, m, wmean[0:r, k:k + 1], None, ALU.subtract)
            then(dve, last)
            then(dve, dve.tensor_scalar(bmean[:], bmean[:], 1.0 / D, None, ALU.mult))
            dve.tensor_tensor(biases[:], biases[:], bmean[:].rearrange("p (k a) -> p k a", a=1).broadcast_to(
                [P, 3 * LAYERS, D]), ALU.subtract).then_inc(centred, 1)

        def block_weights(sp):
            sp.wait_ge(centred, 1)
            for l in range(LAYERS):
                for t in range(8):
                    sp.dma_start(we_diag[E16 * t:E16 * (t + 1), l, D * t:D * (t + 1)],
                                 we[:, l, :]).then_inc(blocks_in, 16)
                for t in range(2):
                    sp.dma_start(wm2_diag[D * t:D * (t + 1), l, D * t:D * (t + 1)],
                                 wm2[:, l, :]).then_inc(blocks_in, 16)
            sp.wait_ge(blocks_in, 16 * (10 * LAYERS + 10))

        def scatter(k):
            width, target, a32 = ((RA, by_dst, A32), (RB, by_src, 2))[k]
            staged = [sem(f"staged{k}_{i}") for i in range(2)]
            rec_ready = [sem(f"rec_ready{k}_{i}") for i in range(2)]
            scattered = [sem(f"scattered{k}_{i}") for i in range(2)]
            tail_done = sem(f"tail_done{k}")
            act_step = sem(f"rec_step{k}")
            e16_c = ea16[0:P * CF, :].rearrange("(p c) f -> p c f", p=P)
            e32_c = ea32[0:P * CF, :].rearrange("(p c) f -> p c f", p=P)
            loads = 1 if k else 2
            copies = 5 - k
            rec = [r[:].rearrange("p c f -> p (c f)")[:, 0:CH * width].rearrange("p (c f) -> p c f", f=width)
                   for r in recs]

            with nc.Block() as block:
                @block.sync
                def _(sp):
                    def load(h, i, first):
                        if not first:
                            sp.wait_ge(rec_ready[h], i * copies)
                        cols = bass.ds((2 * i + h) * CH, CH)
                        if k == 0:
                            sp.dma_start(st16[h][:], e16_c[:, cols, :]).then_inc(staged[h], 16)
                        sp.dma_start(st32[h][:], e32_c[:, cols, :]).then_inc(staged[h], 16)

                    load(0, 0, True)
                    load(1, 0, True)
                    with sp.Fori(1, NCH) as i:
                        load(0, i, False)
                        load(1, i, False)
                    sp.wait_ge(rec_ready[0], NCH * copies)
                    if k == 0:
                        sp.dma_start(st16[0][0:TAIL, 0, :], ea16[P * CF:, :]).then_inc(staged[0], 16)
                    sp.dma_start(st32[0][0:TAIL, 0, :], ea32[P * CF:, :]).then_inc(staged[0], 16)
                    if k == 0:
                        block_weights(sp)
                        rank_windows(sp, 1)

                @block.scalar
                def _(act):
                    if k == 0:
                        for r in rec:
                            act.activation(r[:, :, RA - 2], ones[:, 0:CH], ACT.Copy)
                            act.activation(r[:, :, RA - 1], ones[:, 0:CH], ACT.Copy, scale=0.0).then_inc(act_step, 1)
                    act.activation(key_f[:], keys_i[k][:], ACT.Copy).then_inc(act_step, 1)
                    act.wait_ge(act_step, 3 if k == 0 else 1)

                    def records(h, n, lanes, cols, count, i=None):
                        act.wait_ge(staged[h], 16 * loads * n)
                        if i is not None:
                            act.wait_ge(scattered[h], 16 * CH * i)
                        if k == 0:
                            act.activation(rec[h][0:lanes, 0:count, A16:A16 + E16], st16[h][0:lanes, 0:count, :],
                                           ACT.Copy).then_inc(rec_ready[h], 1)
                        act.activation(rec[h][0:lanes, 0:count, a32:a32 + E32], st32[h][0:lanes, 0:count, :],
                                       ACT.Copy).then_inc(rec_ready[h], 1)
                        act.activation(rec[h][0:lanes, 0:count, 0], key_f[0:lanes, cols],
                                       ACT.Copy).then_inc(rec_ready[h], 1)
                        act.activation(rec[h][0:lanes, 0:count, 1].bitcast(I32), keys_i[1 - k][0:lanes, cols],
                                       ACT.Copy).then_inc(rec_ready[h], 1)
                        act.activation(slots[h][0:lanes, 0:count], place[k][0:lanes, cols],
                                       ACT.Copy).then_inc(rec_ready[h], 1)

                    for h in range(2):
                        records(h, 1, P, bass.ds(h * CH, CH), CH)
                    with act.Fori(1, NCH) as i:
                        for h in range(2):
                            records(h, i + 1, P, bass.ds((2 * i + h) * CH, CH), CH, i)
                    records(0, NCH + 1, TAIL, slice(CF, C), 1, NCH)

                @block.gpsimd
                def _(pool):
                    def write(h, n):
                        pool.wait_ge(rec_ready[h], copies * n)
                        pool.sem_inc(turn, 1)
                        for j in range(CH):
                            pool.indirect_dma_start(
                                out=target, out_offset=bass.IndirectOffsetOnAxis(ap=slots[h][:, j:j + 1], axis=0),
                                in_=rec[h][:, j, :], in_offset=None).then_inc(scattered[h], 16)

                    with pool.Fori(0, NCH) as i:
                        write(0, i + 1)
                        write(1, i + 1)
                    pool.wait_ge(rec_ready[0], copies * (NCH + 1))
                    pool.indirect_dma_start(
                        out=target, out_offset=bass.IndirectOffsetOnAxis(ap=slots[0][0:TAIL, 0:1], axis=0),
                        in_=rec[0][0:TAIL, 0, :], in_offset=None).then_inc(tail_done, 16)
                    pool.wait_ge(scattered[0], 16 * CH * NCH)
                    pool.wait_ge(scattered[1], 16 * CH * NCH)
                    pool.wait_ge(tail_done, 16)

                if k == 0:
                    @block.vector
                    def _(dve):
                        centre_weights(dve)
                        rank_vector(dve, 1)

                    @block.tensor
                    def _(pe):
                        rank_tensor(pe, 1)

        with new_stage():
            scatter(0)
        with new_stage():
            scatter(1)
        order.close()

        far_rows = sb("far_rows", [P, WC, 2 * D])
        NEARB = sb("NEARB", [P, NW, 3, 2 * D], BF16)
        ACC2 = sb("ACC2", [P, NW, E32 + 1])
        NEAR = sb("NEAR", [P, NW, 2 * D])
        ACC = sb("ACC", [P, NW, D])
        H = sb("H", [P, NW, D])
        sqrt_done = sem("sqrt_done")
        sqrt_asked = sem("sqrt_asked")
        n_sqrt = [0]
        S = NEAR[:, :, 0:D]
        mean, rstd = small[:, 0, :], small[:, 1, :]

        def wide(v):
            return v.rearrange("p (w a) -> p w a", a=1).broadcast_to([P, NW, D])

        def over(v):
            return v.rearrange("p (a f) -> p a f", a=1).broadcast_to([P, NW, D])

        def norm_relu(dve, to, frm):
            then(dve, dve.tensor_reduce(mean, frm, AX, ALU.add))
            then(dve, dve.tensor_scalar(mean, mean, 1.0 / D, None, ALU.mult))
            then(dve, dve.tensor_tensor(to, frm, wide(mean), ALU.subtract))
            then(dve, dve.tensor_tensor(S, to, to, ALU.mult))
            then(dve, dve.tensor_reduce(rstd, S, AX, ALU.add))
            then(dve, dve.tensor_scalar(rstd, rstd, 1.0 / D, EPS, ALU.mult, ALU.add))
            root(dve, rstd)
            then(dve, dve.reciprocal(rstd, rstd))
            then(dve, dve.scalar_tensor_tensor(out=to, in0=to, scalar=0.0, in1=wide(rstd), op0=ALU.max, op1=ALU.mult))

        roots = []

        def root(dve, v):
            n_sqrt[0] += 1
            roots.append((v, n_sqrt[0]))
            dve.sem_inc(sqrt_asked, 1)
            dve.wait_ge(sqrt_done, n_sqrt[0])

        def take_roots(act):
            for v, n in roots:
                act.wait_ge(sqrt_asked, n)
                act.activation(v, v, ACT.Sqrt).then_inc(sqrt_done, 1)
            roots.clear()

        def split(dve, rows, width):
            for q in range(3):
                then(dve, dve.tensor_copy(NEARB[:, :, q, 0:width], rows))
                if q < 2:
                    then(dve, dve.tensor_tensor(rows, rows, NEARB[:, :, q, 0:width], ALU.subtract))

        def node_block(steps):
            with nc.Block() as block:
                @block.vector
                def _(dve):
                    steps(dve)

                @block.scalar
                def _(act):
                    take_roots(act)

        def linear(name, weight, width, k_rows, near, near_width, far=None):
            staged, turned = sem(name + "_staged"), sem(name + "_turned")
            turned_in, product, taken = sem(name + "_turned_in"), sem(name + "_product"), sem(name + "_taken")
            far_ready, far_out = sem(name + "_far_ready"), sem(name + "_far_out")
            per = 512 // width
            parts = [(a, min(a + per, WC)) for a in range(0, WC, per)]
            halves = [(0, 4), (4, WC)]
            far_width = width - near_width
            both = 2 if k_rows == P else 1

            with nc.Block() as block:
                @block.vector
                def _(dve):
                    def put(i, n, first):
                        if not first:
                            dve.wait_ge(turned, i)
                        dve.tensor_copy(stage[:, :, 0:D], H[:, bass.ds(i * WC, WC), :]).then_inc(staged, 1)
                        if both == 2:
                            dve.tensor_copy(stage[:, :, D:], ACC[:, bass.ds(i * WC, WC), :]).then_inc(staged, 1)

                    put(0, 1, True)
                    with dve.Fori(1, NWC) as i:
                        put(i, i + 1, False)

                @block.tensor
                def _(pe):
                    def go(n):
                        pe.wait_ge(staged, n * both)
                        for j in range(WC):
                            last = pe.transpose(banks[j // 4][:, (j % 4) * P:(j % 4 + 1) * P], stage[:, j, :], ident[:])
                        last.then_inc(turned, 1)
                        pe.wait_ge(turned_in, 2 * n)
                        for q, (a, b) in enumerate(parts):
                            for j in range(a, b):
                                last = pe.matmul(banks[2 + q][:, (j - a) * width:(j - a + 1) * width],
                                                 lhsT=stage_t[0:k_rows, j, :], rhs=weight, start=True, stop=True)
                        last.then_inc(product, 1)

                    go(1)
                    with pe.Fori(1, NWC) as i:
                        pe.wait_ge(taken, i)
                        go(i + 1)

                @block.scalar
                def _(act):
                    def go(i, n, first):
                        act.wait_ge(turned, n)
                        for q, (a, b) in enumerate(halves):
                            act.activation(stage_t[:, a:b, :].rearrange("p j f -> p (j f)"),
                                           banks[q][:, 0:(b - a) * P], ACT.Copy).then_inc(turned_in, 1)
                        act.wait_ge(product, n)
                        if far is not None and not first:
                            act.wait_ge(far_out, 16 * i)
                        for q, (a, b) in enumerate(parts):
                            rows = banks[2 + q][:, 0:(b - a) * width].rearrange("p (j f) -> p j f", f=width)
                            last = act.activation(near[:, bass.ds(i * WC + a, b - a), 0:near_width],
                                                  rows[:, :, 0:near_width], ACT.Copy)
                            if far is not None:
                                act.activation(far_rows[:, a:b, 0:far_width], rows[:, :, near_width:],
                                               ACT.Copy).then_inc(far_ready, 1)
                        act.activation(act_mark[:], ones[:, 0:1], ACT.Copy).then_inc(taken, 1)

                    go(0, 1, True)
                    with act.Fori(1, NWC) as i:
                        go(i, i + 1, False)

                if far is not None:
                    @block.sync
                    def _(sp):
                        rows = far.rearrange("(w p) f -> p w f", p=P)
                        with sp.Fori(0, NWC) as i:
                            sp.wait_ge(far_ready, (i + 1) * len(parts))
                            sp.dma_start(rows[:, bass.ds(i * WC, WC), :],
                                         far_rows[:, :, 0:far_width]).then_inc(far_out, 16)
                        sp.wait_ge(far_out, 16 * NWC)

        act_mark = sb("act_mark", [P, 1])
        bn = sb("bn", [P, 3, D])

        def rolling(eng, steps, width, last_lag, tick):
            lead = -(-(width + last_lag) // width)
            whole = steps // width

            def at(i, k):
                def part(lag):
                    s = i * width + (k - lag)
                    if isinstance(i, int) and not 0 <= s < steps:
                        return None
                    return (k - lag) % width, s, i * width + (k - lag + 1), i + ((k - lag) // width + 1)
                return part

            for t in range(lead * width):
                tick(at(t // width, t % width))
            with eng.Fori(lead, whole) as i:
                for k in range(width):
                    tick(at(i, k))
            for t in range(whole * width, steps + last_lag):
                tick(at(t // width, t % width))

        def at_least(eng, s, value, scale=1):
            if isinstance(value, int) and value <= 0:
                return
            eng.wait_ge(s, value * scale)

        edge = ExitStack()
        WG = 4
        W2 = 8

        def eb(name, shape, dt=F32, slots=1):
            return [edge.enter_context(nc.sbuf_tensor(f"{name}{h}", shape, dt)) for h in range(slots)]

        rec = eb("rec", [P, 2, GT, RA], F32, WG)
        far_in = eb("far_in", [P, 2 * GT, D], F32, WG)
        onehot = eb("onehot", [P, 2 * GT, P], BF16, WG)
        onehot_t = eb("onehot_t", [P, 2 * GT, P], BF16)
        key_in = eb("key_in", [P, 2 * GT, 4], BF16)
        e_flat = eb("e_flat", [P, P])
        e_t = eb("e_t", [P, P], F32, 2)
        z, = eb("z", [P, 2 * GT, D])
        zz, = eb("zz", [P, 2 * GT, D])
        zr, = eb("zr", [P, 2 * GT, D])
        zr_t, = eb("zr_t", [P, GT, P])
        biased, = eb("biased", [P, 2 * GT, D])
        v, = eb("v", [P, 2 * GT, D])
        vv, = eb("vv", [P, 2 * GT, D])
        pieces = [eb(f"pieces{k}_", [P, 2 * GT, D], BF16)[0] for k in range(3)]
        stat = eb("stat", [P, 6, 2 * GT], F32, WG)
        key_f32, = eb("key_f32", [P, 2 * GT])
        hot_f32 = eb("hot_f32", [P, 2 * GT, P], F32, 2)

        slot_rows = {0: by_dst.rearrange("(g p j) f -> p g (j f)", p=P, j=GT),
                     1: by_src.rearrange("(g p j) f -> p g (j f)", p=P, j=GT)}

        def per_tile(x_, n, width):
            return x_.rearrange("p (t a) -> p t a", a=1).broadcast_to([P, n, width])

        def flat(x_):
            return x_[:].rearrange("p t f -> p (t f)")

        def keys_in_window(dve, to, keys, order_, first, groups):
            n = groups * GT
            base = window_base[:, order_, bass.ds(first, groups)].rearrange("p (g a b) -> p g a b", a=1, b=1)
            return dve.tensor_tensor(to[:, 0:n, :].rearrange("p (g j) c -> p g j c", g=groups), keys,
                                     base.broadcast_to([P, groups, GT, 4]), ALU.subtract)

        def one_hots(dve, to, key, n):
            cols = iota_b[:].rearrange("p (a q c) -> p a q c", a=1, c=4).broadcast_to([P, n, P // 4, 4])
            keys = key[:, 0:n, :].rearrange("p t (a c) -> p t a c", a=1).broadcast_to([P, n, P // 4, 4])
            return dve.tensor_tensor(to[:, 0:n, :].rearrange("p t (q c) -> p t q c", c=4), cols, keys, ALU.is_equal)

        def mpnn_pass(l):
            steps = NG // 2
            s = {n: sem(f"{n}_l{l}") for n in (
                "key_ready", "onehot_ready", "e_ready", "turned", "turned_sb", "h_ps", "z_ready", "square1", "sum1",
                "var1", "root1", "relu_ready", "relu_turned", "relu_t", "v_ps", "bias_ready", "epsvar", "v_ready",
                "square2", "sum2", "var2", "root2", "rec2", "m_ready", "piece0", "rest", "piece1", "piece2", "acc_ps",
                "acc_first", "acc_added")}
            rec_in = [sem(f"rec_in{h}_l{l}") for h in range(WG)]
            far_ready = [sem(f"far_ready{h}_l{l}") for h in range(WG)]
            BE, BH, BR, BV, BA = banks[1], banks[2], banks[3], banks[4], banks[5]
            BO = bank_bf

            with nc.Block() as block:
                @block.sync
                def _(sp):
                    def load(h, i):
                        st = i * WG + h
                        at_least(sp, s["onehot_ready"], st - WG + 1)
                        at_least(sp, s["e_ready"], st - WG + 1)
                        at_least(sp, s["z_ready"], st - WG + 1)
                        sp.dma_start(rec[h][:].rearrange("p g j f -> p g (j f)"),
                                     slot_rows[0][:, bass.ds(2 * st, 2), :]).then_inc(rec_in[h], 16)

                    by_slot(sp, steps, WG, load)

                @block.gpsimd
                def _(pool):
                    def gather(h, i):
                        pool.wait_ge(rec_in[h], 16 * (i + 1))
                        at_least(pool, s["z_ready"], i * WG + h - WG + 1)
                        pool.sem_inc(turn, 1)
                        for t in range(2 * GT):
                            pool.indirect_dma_start(
                                out=far_in[h][:, t, :], out_offset=None, in_=table,
                                in_offset=bass.IndirectOffsetOnAxis(
                                    ap=rec[h][:, t // GT, t % GT, 1:2].bitcast(I32), axis=0),
                            ).then_inc(far_ready[h], 16)

                    by_slot(pool, steps, WG, gather)

                @block.vector
                def _(dve):
                    def tick(part):
                        if p := part(2):
                            h, st, n, nth = p
                            dve.wait_ge(s["root1"], n)
                            dve.tensor_scalar(stat[h][:, 2, :], stat[h][:, 0, :], EPS, None, ALU.mult).then_inc(s["epsvar"], 1)
                            at_least(dve, s["v_ready"], n - 1)
                            dve.tensor_tensor(biased[:], per_tile(stat[h][:, 1, :], 2 * GT, D),
                                              biases[:, LAYERS + l:LAYERS + l + 1, :].broadcast_to([P, 2 * GT, D]),
                                              ALU.mult).then_inc(s["bias_ready"], 1)
                        if p := part(0):
                            h, st, n, nth = p
                            arrived(dve, rec_in, h, nth)
                            at_least(dve, s["onehot_ready"], n - 1)
                            keys_in_window(dve, key_in[0], rec[h][:, :, :, 0:1].broadcast_to([P, 2, GT, 4]),
                                           0, 2 * st, 2).then_inc(s["key_ready"], 1)
                            dve.wait_ge(s["key_ready"], n)
                            at_least(dve, s["acc_ps"], n - WG)
                            one_hots(dve, onehot[h], key_in[0], 2 * GT).then_inc(s["onehot_ready"], 1)
                        if p := part(2):
                            h, st, n, nth = p
                            dve.wait_ge(s["v_ps"], n)
                            dve.wait_ge(s["bias_ready"], n)
                            at_least(dve, s["piece2"], n - 1)
                            dve.tensor_tensor(flat(v), BV[:], flat(biased), ALU.add).then_inc(s["v_ready"], 1)
                        if p := part(3):
                            h, st, n, nth = p
                            w = [dve.value_load(window_of[0:1, 0, bass.ds(2 * st + g, 1)], min_val=0, max_val=NW - 1)
                                 for g in range(2)]
                            dve.wait_ge(s["acc_ps"], n)
                            for g in range(2):
                                row = ACC[:, bass.ds(w[g], 1), :].rearrange("p a f -> p (a f)")
                                mark = s["acc_added" if g else "acc_first"]
                                dve.tensor_tensor(row, row, BA[:, g * D:(g + 1) * D], ALU.add).then_inc(mark, 1)
                                dve.wait_ge(mark, n)
                        if p := part(2):
                            h, st, n, nth = p
                            dve.wait_ge(s["square2"], n)
                            dve.tensor_reduce(stat[h][:, 3, :], vv[:], AX, ALU.add).then_inc(s["sum2"], 1)
                            dve.wait_ge(s["sum2"], n)
                            dve.wait_ge(s["epsvar"], n)
                            dve.scalar_tensor_tensor(out=stat[h][:, 4, :], in0=stat[h][:, 3, :], scalar=1.0 / D,
                                                     in1=stat[h][:, 2, :], op0=ALU.mult, op1=ALU.add).then_inc(s["var2"], 1)
                        if p := part(2):
                            h, st, n, nth = p
                            dve.wait_ge(s["root2"], n)
                            dve.reciprocal(stat[h][:, 5, :], stat[h][:, 4, :]).then_inc(s["rec2"], 1)
                            dve.wait_ge(s["rec2"], n)
                            dve.scalar_tensor_tensor(out=v[:], in0=v[:], scalar=0.0, in1=per_tile(stat[h][:, 5, :], 2 * GT, D),
                                                     op0=ALU.max, op1=ALU.mult).then_inc(s["m_ready"], 1)
                        if p := part(1):
                            h, st, n, nth = p
                            dve.wait_ge(s["h_ps"], n)
                            arrived(dve, far_ready, h, nth, 2 * GT)
                            at_least(dve, s["square1"], n - 1)
                            dve.tensor_tensor(flat(z), BH[:], flat(far_in[h]), ALU.add).then_inc(s["z_ready"], 1)
                        if p := part(2):
                            h, st, n, nth = p
                            dve.wait_ge(s["piece0"], n)
                            dve.tensor_tensor(v[:], v[:], pieces[0][:], ALU.subtract).then_inc(s["rest"], 1)
                        if p := part(1):
                            h, st, n, nth = p
                            dve.wait_ge(s["square1"], n)
                            dve.tensor_reduce(stat[h][:, 0, :], zz[:], AX, ALU.add).then_inc(s["sum1"], 1)
                            dve.wait_ge(s["sum1"], n)
                            dve.tensor_scalar(stat[h][:, 0, :], stat[h][:, 0, :], 1.0 / D, EPS, ALU.mult,
                                              ALU.add).then_inc(s["var1"], 1)
                        if p := part(2):
                            h, st, n, nth = p
                            dve.wait_ge(s["piece1"], n)
                            dve.tensor_tensor(pieces[2][:], v[:], pieces[1][:], ALU.subtract).then_inc(s["piece2"], 1)

                    rolling(dve, steps, WG, 3, tick)

                @block.scalar
                def _(act):
                    act.preload_act_table_set("sqrt_and_friends")

                    def tick(part):
                        if p := part(1):
                            h, st, n, nth = p
                            act.wait_ge(s["turned"], n)
                            at_least(act, s["h_ps"], n - 1)
                            act.activation(flat(onehot_t[0]), BO[:], ACT.Copy)
                            act.activation(e_t[0][:], BE[:, 0:P], ACT.Copy).then_inc(s["turned_sb"], 1)
                        if p := part(0):
                            h, st, n, nth = p
                            arrived(act, rec_in, h, nth)
                            at_least(act, s["turned"], n - 1)
                            act.activation(e_flat[0][:].rearrange("p (g j f) -> p (g j) f", g=2, j=GT),
                                           rec[h][:, :, :, A16:A16 + E16].rearrange("p g j f -> p (g j) f"),
                                           ACT.Copy).then_inc(s["e_ready"], 1)
                        if p := part(2):
                            h, st, n, nth = p
                            act.wait_ge(s["v_ready"], n)
                            at_least(act, s["sum2"], n - 1)
                            act.activation(vv[:], v[:], ACT.Square).then_inc(s["square2"], 1)
                            act.wait_ge(s["var2"], n)
                            act.activation(stat[h][:, 4, :], stat[h][:, 4, :], ACT.Sqrt).then_inc(s["root2"], 1)
                        if p := part(2):
                            h, st, n, nth = p
                            act.wait_ge(s["m_ready"], n)
                            at_least(act, s["acc_ps"], n - 1)
                            act.activation(pieces[0][:], v[:], ACT.Copy).then_inc(s["piece0"], 1)
                        if p := part(1):
                            h, st, n, nth = p
                            act.wait_ge(s["z_ready"], n)
                            at_least(act, s["relu_turned"], n - 1)
                            act.activation(zr[:], z[:], ACT.Relu).then_inc(s["relu_ready"], 1)
                            at_least(act, s["sum1"], n - 1)
                            act.activation(zz[:], z[:], ACT.Square).then_inc(s["square1"], 1)
                        if p := part(2):
                            h, st, n, nth = p
                            act.wait_ge(s["rest"], n)
                            act.activation(pieces[1][:], v[:], ACT.Copy).then_inc(s["piece1"], 1)
                        if p := part(1):
                            h, st, n, nth = p
                            act.wait_ge(s["relu_turned"], n)
                            at_least(act, s["v_ps"], n - 1)
                            act.activation(flat(zr_t), BR[:], ACT.Copy).then_inc(s["relu_t"], 1)
                        if p := part(1):
                            h, st, n, nth = p
                            act.wait_ge(s["var1"], n)
                            act.activation(stat[h][:, 1, :], stat[h][:, 0, :], ACT.Sqrt).then_inc(s["root1"], 1)

                    rolling(act, steps, WG, 2, tick)

                @block.tensor
                def _(pe):
                    def tick(part):
                        if p := part(2):
                            h, st, n, nth = p
                            pe.wait_ge(s["relu_t"], n)
                            at_least(pe, s["v_ready"], n - 1)
                            for q in range(GT):
                                last = pe.matmul(BV[:, q * P:(q + 1) * P], lhsT=zr_t[:, q, :], rhs=wm2_diag[:, l, :],
                                                 start=True, stop=True)
                            last.then_inc(s["v_ps"], 1)
                        if p := part(3):
                            h, st, n, nth = p
                            pe.wait_ge(s["piece2"], n)
                            at_least(pe, s["acc_added"], n - 1)
                            last = sum_pieces(pe, BA, onehot[h], 2, 0)
                            last.then_inc(s["acc_ps"], 1)
                        if p := part(1):
                            h, st, n, nth = p
                            w = [pe.value_load(window_of[0:1, 0, bass.ds(2 * st + g, 1)], min_val=0, max_val=NW - 1)
                                 for g in range(2)]
                            pe.wait_ge(s["turned_sb"], n)
                            at_least(pe, s["z_ready"], n - 1)
                            pe.matmul(BH[:], lhsT=e_t[0][:], rhs=we_diag[:, l, :], start=True, stop=False,
                                      skip_group_check=True)
                            for g in range(2):
                                for j in range(GT):
                                    t = g * GT + j
                                    for q in range(3):
                                        last = pe.matmul(BH[:, t * D:(t + 1) * D], lhsT=onehot_t[0][:, t, :],
                                                         rhs=NEARB[:, bass.ds(w[g], 1), q, 0:D].rearrange("p a f -> p (a f)"),
                                                         start=False, stop=q == 2, skip_group_check=True)
                            last.then_inc(s["h_ps"], 1)
                        if p := part(0):
                            h, st, n, nth = p
                            pe.wait_ge(s["e_ready"], n)
                            at_least(pe, s["turned_sb"], n - 1)
                            pe.transpose(BE[:, 0:P], e_flat[0][:], ident[:])
                            pe.wait_ge(s["onehot_ready"], n)
                            for t in range(2 * GT):
                                last = pe.transpose(BO[:, t * P:(t + 1) * P], onehot[h][:, t, :], ident_b[:])
                            last.then_inc(s["turned"], 1)
                        if p := part(1):
                            h, st, n, nth = p
                            pe.wait_ge(s["relu_ready"], n)
                            at_least(pe, s["relu_t"], n - 1)
                            for q in range(GT):
                                last = pe.transpose(BR[:, q * P:(q + 1) * P],
                                                    zr[:, 2 * q:2 * q + 2, :].rearrange("p t f -> p (t f)"), ident[:])
                            last.then_inc(s["relu_turned"], 1)

                    rolling(pe, steps, WG, 3, tick)

        def sum_pieces(pe, bank, hot, groups, offset):
            for g in range(groups):
                for j in range(GT):
                    for q in range(3):
                        last = pe.matmul(bank[:, g * D:(g + 1) * D], lhsT=hot[:, g * GT + j, :],
                                         rhs=pieces[q][:, offset + g * GT + j, :], start=(j == 0 and q == 0),
                                         stop=(j == GT - 1 and q == 2))
            return last

        def arrived(eng, dma_sems, h, nth, parts=1):
            eng.wait_ge(dma_sems[h], nth * 16 * parts)

        def by_slot(eng, steps, width, f):
            for h in range(width):
                f(h, 0)
            with eng.Fori(1, steps // width) as i:
                for h in range(width):
                    f(h, i)
            for h in range(steps % width):
                f(h, steps // width)

        def gate_pass():
            steps = NG
            s = {n: sem(f"gate_{n}") for n in (
                "key_ready", "onehot_ready", "e_ready", "turned", "turned_sb", "h_ps", "z_ready", "neg", "exps", "logs",
                "log_sig", "soft", "sig", "m_ready", "piece0", "rest", "piece1", "piece2", "acc_ps", "acc_added")}
            rec_in = [sem(f"gate_rec_in{h}") for h in range(W2)]
            far_ready = [sem(f"gate_far_ready{h}") for h in range(W2)]
            BH, BA = [banks[2], banks[3]], [banks[4], banks[5]]
            BE, BO = [banks[0][:, 0:P], banks[1][:, 0:P]], [bank_bf[:, k * GT * P:(k + 1) * GT * P] for k in range(2)]
            hot_t = [onehot_t[0][:, k * GT:(k + 1) * GT, :] for k in range(2)]
            zs = [z, biased]
            logs = [zz, zr]
            soft, sig, m = v[:, 0:GT, :], v[:, GT:, :], [vv[:, 0:GT, :], vv[:, GT:, :]]
            hot = [x_[:, k * GT:(k + 1) * GT, :] for x_ in onehot for k in range(2)]
            recb = [x_[:].rearrange("p g j f -> p (g j f)")[:, k * GT * RB:(k + 1) * GT * RB]
                    .rearrange("p (j f) -> p j f", f=RB) for x_ in rec for k in range(2)]
            piece = [[x_[:, k * GT:(k + 1) * GT, :] for x_ in pieces] for k in range(2)]

            def halves(x_):
                x4 = x_[:].rearrange("p (t k) f -> p t k f", k=2)
                return x4[:, :, 0, :], x4[:, :, 1, :]

            with nc.Block() as block:
                @block.sync
                def _(sp):
                    def load(h, i):
                        st = i * W2 + h
                        at_least(sp, s["onehot_ready"], st - W2 + 1)
                        at_least(sp, s["e_ready"], st - W2 + 1)
                        at_least(sp, s["z_ready"], st - W2 + 1)
                        sp.dma_start(recb[h].rearrange("p j f -> p (j f)"),
                                     slot_rows[1][:, bass.ds(st, 1), :].rearrange("p a f -> p (a f)")
                                     ).then_inc(rec_in[h], 16)

                    by_slot(sp, steps, W2, load)

                @block.gpsimd
                def _(pool):
                    def gather(h, i):
                        pool.wait_ge(rec_in[h], 16 * (i + 1))
                        at_least(pool, s["z_ready"], i * W2 + (h - 4 + 1))
                        pool.sem_inc(turn, 1)
                        for t in range(GT):
                            pool.indirect_dma_start(
                                out=far_in[h % 4][:, 2 * t:2 * t + 2, :].rearrange("p t f -> p (t f)"), out_offset=None,
                                in_=table2, in_offset=bass.IndirectOffsetOnAxis(
                                    ap=recb[h][:, t, 1:2].bitcast(I32), axis=0)).then_inc(far_ready[h], 16)

                    by_slot(pool, steps, W2, gather)

                @block.vector
                def _(dve):
                    def tick(part):
                        if p := part(2):
                            h, st, n, nth = p
                            dve.wait_ge(s["h_ps"], n)
                            arrived(dve, far_ready, h, nth, GT)
                            at_least(dve, s["soft"], n - 2)
                            dve.tensor_tensor(flat(zs[h % 2]), BH[h % 2][:], flat(far_in[h % 4]), ALU.add).then_inc(s["z_ready"], 1)
                            dve.wait_ge(s["z_ready"], n)
                            dve.scalar_tensor_tensor(out=logs[h % 2][:], in0=zs[h % 2][:], scalar=-1.0, in1=zs[h % 2][:],
                                                     op0=ALU.mult, op1=ALU.min).then_inc(s["neg"], 1)
                        if p := part(0):
                            h, st, n, nth = p
                            arrived(dve, rec_in, h, nth)
                            at_least(dve, s["onehot_ready"], n - 1)
                            keys_in_window(dve, key_in[0], recb[h][:, :, 0:1].rearrange(
                                "p (g j) c -> p g j c", g=1).broadcast_to([P, 1, GT, 4]), 1, st, 1).then_inc(s["key_ready"], 1)
                            dve.wait_ge(s["key_ready"], n)
                            at_least(dve, s["acc_ps"], n - W2)
                            one_hots(dve, hot[h], key_in[0], GT).then_inc(s["onehot_ready"], 1)
                        if p := part(3):
                            h, st, n, nth = p
                            dve.wait_ge(s["logs"], n)
                            at_least(dve, s["m_ready"], n - 1)
                            (f, sp_), (lf, ls) = halves(zs[h % 2]), halves(logs[h % 2])
                            dve.scalar_tensor_tensor(out=sig, in0=f, scalar=0.0, in1=lf, op0=ALU.min,
                                                     op1=ALU.subtract).then_inc(s["log_sig"], 1)
                            dve.scalar_tensor_tensor(out=soft, in0=sp_, scalar=0.0, in1=ls, op0=ALU.max,
                                                     op1=ALU.add).then_inc(s["soft"], 1)
                        if p := part(4):
                            h, st, n, nth = p
                            dve.wait_ge(s["piece0"], n)
                            dve.tensor_tensor(m[h % 2], m[h % 2], piece[h % 2][0], ALU.subtract).then_inc(s["rest"], 1)
                        if p := part(3):
                            h, st, n, nth = p
                            dve.wait_ge(s["soft"], n)
                            dve.wait_ge(s["sig"], n)
                            at_least(dve, s["piece2"], n - 2)
                            dve.tensor_tensor(m[h % 2], soft, sig, ALU.mult).then_inc(s["m_ready"], 1)
                        if p := part(4):
                            h, st, n, nth = p
                            dve.wait_ge(s["piece1"], n)
                            dve.tensor_tensor(piece[h % 2][2], m[h % 2], piece[h % 2][1],
                                              ALU.subtract).then_inc(s["piece2"], 1)
                        if p := part(6):
                            h, st, n, nth = p
                            w = dve.value_load(window_of[0:1, 1, bass.ds(st, 1)], min_val=0, max_val=NW - 1)
                            dve.wait_ge(s["acc_ps"], n)
                            at_least(dve, s["acc_added"], n - 1)
                            row = ACC[:, bass.ds(w, 1), :].rearrange("p a f -> p (a f)")
                            dve.tensor_tensor(row, row, BA[h % 2][:, 0:D], ALU.add).then_inc(s["acc_added"], 1)

                    rolling(dve, steps, W2, 6, tick)

                @block.scalar
                def _(act):
                    act.preload_act_table_set("natural_log_exp_and_others")

                    def tick(part):
                        if p := part(1):
                            h, st, n, nth = p
                            act.wait_ge(s["turned"], n)
                            at_least(act, s["h_ps"], n - 2)
                            act.activation(hot_t[h % 2].rearrange("p t n -> p (t n)"), BO[h % 2], ACT.Copy)
                            act.activation(e_t[h % 2][:], BE[h % 2], ACT.Copy).then_inc(s["turned_sb"], 1)
                        if p := part(0):
                            h, st, n, nth = p
                            arrived(act, rec_in, h, nth)
                            at_least(act, s["turned"], n - 1)
                            act.activation(e_flat[0][:].rearrange("p (j f) -> p j f", j=GT), recb[h][:, :, 2:2 + E32],
                                           ACT.Copy).then_inc(s["e_ready"], 1)
                        if p := part(2):
                            h, st, n, nth = p
                            act.wait_ge(s["neg"], n)
                            act.activation(logs[h % 2][:], logs[h % 2][:], ACT.Exp).then_inc(s["exps"], 1)
                            act.wait_ge(s["exps"], n)
                            act.activation(logs[h % 2][:], logs[h % 2][:], ACT.Ln, bias=1.0).then_inc(s["logs"], 1)
                        if p := part(3):
                            h, st, n, nth = p
                            act.wait_ge(s["log_sig"], n)
                            act.activation(sig, sig, ACT.Exp).then_inc(s["sig"], 1)
                        if p := part(4):
                            h, st, n, nth = p
                            act.wait_ge(s["rest"], n)
                            act.activation(piece[h % 2][1], m[h % 2], ACT.Copy).then_inc(s["piece1"], 1)
                        if p := part(3):
                            h, st, n, nth = p
                            act.wait_ge(s["m_ready"], n)
                            at_least(act, s["acc_ps"], n - 2)
                            act.activation(piece[h % 2][0], m[h % 2], ACT.Copy).then_inc(s["piece0"], 1)

                    rolling(act, steps, W2, 4, tick)

                @block.tensor
                def _(pe):
                    def tick(part):
                        if p := part(5):
                            h, st, n, nth = p
                            pe.wait_ge(s["piece2"], n)
                            at_least(pe, s["acc_added"], n - 2)
                            sum_pieces(pe, BA[h % 2], hot[h], 1, (h % 2) * GT).then_inc(s["acc_ps"], 1)
                        if p := part(1):
                            h, st, n, nth = p
                            w = pe.value_load(window_of[0:1, 1, bass.ds(st, 1)], min_val=0, max_val=NW - 1)
                            pe.wait_ge(s["turned_sb"], n)
                            at_least(pe, s["z_ready"], n - 2)
                            bank = BH[h % 2]
                            pe.matmul(bank[:], lhsT=e_t[h % 2][:], rhs=wge_diag[:], start=True, stop=False, skip_group_check=True)
                            for t in range(GT):
                                for q in range(3):
                                    last = pe.matmul(bank[:, t * 2 * D:(t + 1) * 2 * D], lhsT=hot_t[h % 2][:, t, :],
                                                     rhs=NEARB[:, bass.ds(w, 1), q, :].rearrange("p a f -> p (a f)"),
                                                     start=False, stop=q == 2, skip_group_check=True)
                            last.then_inc(s["h_ps"], 1)
                        if p := part(0):
                            h, st, n, nth = p
                            pe.wait_ge(s["e_ready"], n)
                            at_least(pe, s["turned_sb"], n - 2)
                            pe.transpose(BE[h % 2], e_flat[0][:], ident[:])
                            pe.wait_ge(s["onehot_ready"], n)
                            for t in range(GT):
                                last = pe.transpose(BO[h % 2][:, t * P:(t + 1) * P], hot[h][:, t, :], ident_b[:])
                            last.then_inc(s["turned"], 1)

                    rolling(pe, steps, W2, 5, tick)

        def sum_pass(name, with_edges):
            steps = NG // 2
            s = {n: sem(f"{name}_{n}") for n in (
                "key_ready", "onehot_ready", "acc_ps", "acc_first", "acc_added", "acc2_first", "acc2_added")}
            rec_in = [sem(f"{name}_rec_in{h}") for h in range(WG)]
            far_ready = [sem(f"{name}_far_ready{h}") for h in range(WG)]
            EW = E32 + 1

            with nc.Block() as block:
                @block.sync
                def _(sp):
                    def load(h, i):
                        st = i * WG + h
                        at_least(sp, s["acc_ps"], st - WG + 1)
                        sp.dma_start(rec[h][:].rearrange("p g j f -> p g (j f)"),
                                     slot_rows[0][:, bass.ds(2 * st, 2), :]).then_inc(rec_in[h], 16)

                    by_slot(sp, steps, WG, load)

                @block.gpsimd
                def _(pool):
                    def gather(h, i):
                        pool.wait_ge(rec_in[h], 16 * (i + 1))
                        at_least(pool, s["acc_ps"], i * WG + h - WG + 1)
                        pool.sem_inc(turn, 1)
                        for t in range(2 * GT):
                            pool.indirect_dma_start(
                                out=far_in[h][:, t, :], out_offset=None, in_=table,
                                in_offset=bass.IndirectOffsetOnAxis(
                                    ap=rec[h][:, t // GT, t % GT, 1:2].bitcast(I32), axis=0),
                            ).then_inc(far_ready[h], 16)

                    by_slot(pool, steps, WG, gather)

                @block.vector
                def _(dve):
                    def tick(part):
                        if p := part(0):
                            h, st, n, nth = p
                            arrived(dve, rec_in, h, nth)
                            at_least(dve, s["onehot_ready"], n - 1)
                            base = window_base[:, 0, bass.ds(2 * st, 2)].rearrange("p (g a) -> p g a", a=1)
                            dve.tensor_tensor(key_f32[:].rearrange("p (g j) -> p g j", g=2), rec[h][:, :, :, 0],
                                              base.broadcast_to([P, 2, GT]), ALU.subtract).then_inc(s["key_ready"], 1)
                            dve.wait_ge(s["key_ready"], n)
                            at_least(dve, s["acc_ps"], n - 2)
                            dve.tensor_tensor(hot_f32[h % 2][:], iota_f[:].rearrange("p (a n) -> p a n", a=1)
                                              .broadcast_to([P, 2 * GT, P]), per_tile(key_f32[:], 2 * GT, P),
                                              ALU.is_equal).then_inc(s["onehot_ready"], 1)
                        if p := part(2):
                            h, st, n, nth = p
                            w = [dve.value_load(window_of[0:1, 0, bass.ds(2 * st + g, 1)], min_val=0, max_val=NW - 1)
                                 for g in range(2)]
                            dve.wait_ge(s["acc_ps"], n)
                            for g in range(2):
                                row = ACC[:, bass.ds(w[g], 1), :].rearrange("p a f -> p (a f)")
                                mark = s["acc_added" if g else "acc_first"]
                                dve.tensor_tensor(row, row, banks[2 * (h % 2)][:, g * D:(g + 1) * D], ALU.add).then_inc(mark, 1)
                                dve.wait_ge(mark, n)
                                if with_edges:
                                    row = ACC2[:, bass.ds(w[g], 1), :].rearrange("p a f -> p (a f)")
                                    mark = s["acc2_added" if g else "acc2_first"]
                                    dve.tensor_tensor(row, row, banks[2 * (h % 2) + 1][:, g * EW:(g + 1) * EW], ALU.add).then_inc(mark, 1)
                                    dve.wait_ge(mark, n)

                    rolling(dve, steps, WG, 2, tick)

                @block.tensor
                def _(pe):
                    def tick(part):
                        if p := part(1):
                            h, st, n, nth = p
                            hot = hot_f32[h % 2]
                            pe.wait_ge(s["onehot_ready"], n)
                            at_least(pe, s["acc2_added" if with_edges else "acc_added"], n - 2)
                            arrived(pe, rec_in, h, nth)
                            for g in range(2 if with_edges else 0):
                                for j in range(GT):
                                    pe.matmul(banks[2 * (h % 2) + 1][:, g * EW:(g + 1) * EW], lhsT=hot[:, g * GT + j, :],
                                              rhs=rec[h][:, g, j, A32:A32 + EW], start=(j == 0), stop=(j == GT - 1))
                            arrived(pe, far_ready, h, nth, 2 * GT)
                            for g in range(2):
                                for j in range(GT):
                                    last = pe.matmul(banks[2 * (h % 2)][:, g * D:(g + 1) * D], lhsT=hot[:, g * GT + j, :],
                                                     rhs=far_in[h][:, g * GT + j, :], start=(j == 0), stop=(j == GT - 1))
                            last.then_inc(s["acc_ps"], 1)

                    rolling(pe, steps, WG, 1, tick)

        node_block(lambda dve: norm_relu(dve, H[:], X[:]))
        for l in range(LAYERS):
            with new_stage():
                linear(f"tables{l}", wtab[:, l, :], 2 * D, D, NEAR, D, table)

            def before_edges(dve, l=l):
                then(dve, dve.tensor_tensor(S, S, over(biases[:, l, :]), ALU.add))
                split(dve, S, D)
                then(dve, dve.memset(ACC[:], 0.0))
            node_block(before_edges)
            with new_stage():
                mpnn_pass(l)
            with new_stage():
                linear(f"update{l}", wupd[:, l, :], D, P, NEAR[:, :, D:], D)

            def update(dve, l=l):
                T = NEAR[:, :, D:]
                then(dve, dve.tensor_tensor(T, T, over(biases[:, 2 * LAYERS + l, :]), ALU.add))
                norm_relu(dve, ACC[:], T)
                then(dve, dve.tensor_tensor(H[:], H[:], ACC[:], ALU.add))
                if l == LAYERS - 1:
                    then(dve, dve.tensor_tensor(X[:], X[:], H[:], ALU.add))
                    norm_relu(dve, H[:], X[:])
            node_block(update)

        with new_stage():
            linear("gate_tables", wgate[:], 4 * D, D, NEAR, 2 * D, table2)

        def before_gate(dve):
            then(dve, dve.tensor_tensor(
                NEAR[:], NEAR[:], gate_bias[:].rearrange("p k f -> p (k f)").rearrange("p (a f) -> p a f", a=1)
                .broadcast_to([P, NW, 2 * D]), ALU.add))
            split(dve, NEAR[:], 2 * D)
            then(dve, dve.memset(ACC[:], 0.0))
        node_block(before_gate)
        with new_stage():
            gate_pass()

        bn_asked, bn_done = sem("bn_asked"), sem("bn_done")
        table_ready, table_out = sem("table_ready"), sem("table_out")

        def send_state(sp, n):
            sp.wait_ge(table_ready, n)
            sp.dma_start(table.rearrange("(w p) f -> p w f", p=P), H[:]).then_inc(table_out, 16)
            sp.wait_ge(table_out, 16 * n)

        with nc.Block() as block:
            @block.tensor
            def _(pe):
                for n in range(2):
                    pe.wait_ge(bn_asked, n + 1)
                    pe.matmul(banks[n][:, 0:D], lhsT=ones[:], rhs=bn[:, n, :], start=True, stop=True).then_inc(bn_done, 1)

            @block.vector
            def _(dve):
                dve.tensor_reduce(bn[:, 0, :], ACC[:].rearrange("p w f -> p f w"), AX, ALU.add).then_inc(bn_asked, 1)
                dve.wait_ge(bn_done, 1)
                then(dve, dve.tensor_scalar(bn[:, 2, :], banks[0][:, 0:D], 1.0 / N, None, ALU.mult))
                then(dve, dve.tensor_tensor(ACC[:], ACC[:], over(bn[:, 2, :]), ALU.subtract))
                then(dve, dve.tensor_scalar(ACC[:, NW - 1, :], ACC[:, NW - 1, :], valid[:, 0:1], None, ALU.mult))
                then(dve, dve.tensor_tensor(S, ACC[:], ACC[:], ALU.mult))
                dve.tensor_reduce(bn[:, 1, :], S.rearrange("p w f -> p f w"), AX, ALU.add).then_inc(bn_asked, 1)
                dve.wait_ge(bn_done, 2)
                then(dve, dve.tensor_scalar(bn[:, 2, :], banks[1][:, 0:D], 1.0 / N, EPS, ALU.mult, ALU.add))
                root(dve, bn[:, 2, :])
                then(dve, dve.reciprocal(bn[:, 2, :], bn[:, 2, :]))
                then(dve, dve.tensor_tensor(bn[:, 2, :], bn[:, 2, :], gb[:, 0, :], ALU.mult))
                then(dve, dve.tensor_tensor(ACC[:], ACC[:], over(bn[:, 2, :]), ALU.mult))
                then(dve, dve.tensor_tensor(ACC[:], ACC[:], over(gb[:, 1, :]), ALU.add))
                then(dve, dve.tensor_tensor(ACC[:], ACC[:], H[:], ALU.add))
                then(dve, dve.tensor_tensor(X[:], X[:], ACC[:], ALU.add))
                norm_relu(dve, H[:], X[:])
                dve.memset(ACC[:], 0.0).then_inc(table_ready, 1)

            @block.scalar
            def _(act):
                take_roots(act)

            @block.sync
            def _(sp):
                send_state(sp, 1)

        with new_stage():
            sum_pass("sum", False)

        with nc.Block() as block:
            @block.vector
            def _(dve):
                then(dve, dve.tensor_tensor(X[:], X[:], ACC[:], ALU.add))
                norm_relu(dve, H[:], X[:])
                then(dve, dve.memset(ACC2[:], 0.0))
                dve.memset(ACC[:], 0.0).then_inc(table_ready, 1)

            @block.scalar
            def _(act):
                take_roots(act)

            @block.sync
            def _(sp):
                send_state(sp, 2)

        with new_stage():
            sum_pass("last", True)

        edge.close()
        staged, turned, turned_in = sem("out_staged"), sem("out_turned"), sem("out_turned_in")
        turned2, turned2_in = sem("out_turned2"), sem("out_turned2_in")
        hidden, hidden_in, product, summed = sem("out_hidden"), sem("out_hidden_in"), sem("out_product"), sem("out_summed")
        out_done = sem("out_done")
        stage2 = sb("stage2", [P, WC, E32 + 1])
        stage2_t = sb("stage2_t", [E32 + 1, WC, P])
        acc_t = sb("acc_t", [D, WC, P])
        hidden_t = sb("hidden_t", [P, WC, P])
        HALVES = [(0, 4), (4, WC)]
        EW = E32 + 1

        with nc.Block() as block:
            @block.vector
            def _(dve):
                def put(i, n, first):
                    if not first:
                        dve.wait_ge(turned, i)
                        dve.wait_ge(turned2, i)
                    dve.tensor_copy(stage[:, :, 0:D], H[:, bass.ds(i * WC, WC), :]).then_inc(staged, 1)
                    dve.tensor_copy(stage[:, :, D:], ACC[:, bass.ds(i * WC, WC), :]).then_inc(staged, 1)
                    dve.tensor_copy(stage2[:], ACC2[:, bass.ds(i * WC, WC), :]).then_inc(staged, 1)
                    dve.wait_ge(product, n)
                    dve.tensor_tensor(S[:, bass.ds(i * WC, WC), :], X[:, bass.ds(i * WC, WC), :],
                                      banks[6][:, 0:WC * D].rearrange("p (j f) -> p j f", f=D),
                                      ALU.add).then_inc(summed, 1)

                put(0, 1, True)
                with dve.Fori(1, NWC) as i:
                    put(i, i + 1, False)
                dve.wait_ge(summed, NWC)
                dve.tensor_tensor(S, S, over(c2r[:]), ALU.add).then_inc(out_done, 1)

            @block.tensor
            def _(pe):
                def go(n):
                    pe.wait_ge(staged, 3 * n)
                    for j in range(WC):
                        last = pe.transpose(banks[j // 4][:, (j % 4) * P:(j % 4 + 1) * P], stage[:, j, :], ident[:])
                    last.then_inc(turned, 1)
                    for j in range(WC):
                        last = pe.transpose(banks[2 + j // 4][0:EW, (j % 4) * P:(j % 4 + 1) * P], stage2[:, j, :], ident[:])
                    last.then_inc(turned2, 1)
                    pe.wait_ge(turned_in, 6 * n)
                    for q, (a, b) in enumerate(HALVES):
                        pe.matmul(banks[4 + q][:, 0:(b - a) * P], lhsT=v1a[:],
                                  rhs=acc_t[:, a:b, :].rearrange("p j f -> p (j f)"), start=True, stop=False)
                        last = pe.matmul(banks[4 + q][:, 0:(b - a) * P], lhsT=v1b[:],
                                         rhs=stage2_t[:, a:b, :].rearrange("p j f -> p (j f)"), start=False, stop=True)
                    last.then_inc(hidden, 1)
                    pe.wait_ge(hidden_in, 2 * n)
                    for j in range(WC):
                        pe.matmul(banks[6][:, j * D:(j + 1) * D], lhsT=stage_t[0:D, j, :], rhs=v2a[:], start=True, stop=False)
                        last = pe.matmul(banks[6][:, j * D:(j + 1) * D], lhsT=hidden_t[:, j, :], rhs=v2b[:],
                                         start=False, stop=True)
                    last.then_inc(product, 1)

                go(1)
                with pe.Fori(1, NWC) as i:
                    pe.wait_ge(summed, i)
                    go(i + 1)

            @block.scalar
            def _(act):
                with act.Fori(0, NWC) as i:
                    n = i + 1
                    act.wait_ge(turned, n)
                    act.wait_ge(turned2, n)
                    for q, (a, b) in enumerate(HALVES):
                        act.activation(stage_t[0:D, a:b, :].rearrange("p j f -> p (j f)"),
                                       banks[q][0:D, 0:(b - a) * P], ACT.Copy).then_inc(turned_in, 1)
                        act.activation(acc_t[:, a:b, :].rearrange("p j f -> p (j f)"),
                                       banks[q][D:P, 0:(b - a) * P], ACT.Copy).then_inc(turned_in, 1)
                        act.activation(stage2_t[:, a:b, :].rearrange("p j f -> p (j f)"),
                                       banks[2 + q][0:EW, 0:(b - a) * P], ACT.Copy).then_inc(turned_in, 1)
                    act.wait_ge(hidden, n)
                    for q, (a, b) in enumerate(HALVES):
                        act.activation(hidden_t[:, a:b, :].rearrange("p j f -> p (j f)"),
                                       banks[4 + q][:, 0:(b - a) * P], ACT.Copy).then_inc(hidden_in, 1)

            @block.sync
            def _(sp):
                sp.wait_ge(out_done, 1)
                sp.dma_start(out[0:(NW - 1) * P, :].rearrange("(w p) f -> p w f", p=P), S[:, 0:NW - 1, :]).then_inc(table_out, 16)
                sp.dma_start(out[(NW - 1) * P:, :], S[0:LASTW, NW - 1, :]).then_inc(table_out, 16)
                sp.wait_ge(table_out, 64)


_INS = ['x', 'src', 'dst', 'edge_attr_16', 'edge_attr_32', 'L0_gnn_msg_w1', 'L0_gnn_msg_b1', 'L0_gnn_msg_w2',
        'L0_gnn_msg_b2', 'L0_gnn_upd_w', 'L0_gnn_upd_b', 'L1_gnn_W_f', 'L1_gnn_b_f', 'L1_gnn_W_s', 'L1_gnn_b_s',
        'L1_gnn_gamma', 'L1_gnn_beta', 'L3_gnn_W1', 'L3_gnn_b1', 'L3_gnn_W2', 'L3_gnn_b2']


def kernel(**inputs):
    import numpy as _np
    import concourse.bacc as _bacc
    from concourse import mybir as _mybir
    from concourse.bass_utils import run_bass_kernel_spmd as _run

    nc = _bacc.Bacc("TRN2", target_bir_lowering=False, num_devices=1)
    arrays, args = {}, []
    for name in _INS:
        a = _np.ascontiguousarray(inputs[name])
        arrays[f"in_{name}"] = a
        args.append(nc.dram_tensor(f"in_{name}", a.shape, _mybir.dt.from_np(a.dtype), kind="ExternalInput").ap())
    args.append(nc.dram_tensor("out_x", (N, D), F32, kind="ExternalOutput").ap())
    build(nc, *args)
    r = _run(nc, [arrays], core_ids=[0])
    return r.results[0]["out_x"]
```
